# Optimizing a Trainium2 kernel written in Bass

```python
import numpy as np
import jax
import jax.numpy as jnp

def _softmax(x, axis=-1):
    return jax.nn.softmax(x, axis=axis)

def _gelu(x):
    return jax.nn.gelu(x, approximate=True)

def _silu(x):
    return jax.nn.silu(x)

def _sigmoid(x):
    return jax.nn.sigmoid(x)

def _layernorm(x, axis=-1, eps=1e-05):
    m = jnp.mean(x, axis=axis, keepdims=True)
    v = jnp.var(x, axis=axis, keepdims=True)
    return (x - m) / jnp.sqrt(v + eps)

def _scatter_add(tgt, idx, src, axis=0):
    return tgt.at[idx].add(src)

def _segment_sum(src, seg, n):
    return jax.ops.segment_sum(src, seg, n)
kernel_name = 'mk_pixart_resid_d1_seqx_r4_155dff'

def setup_inputs(seed: int=0):
    np.random.seed(seed)
    _w = jnp.asarray

    def _rec_inputs():
        import jax
        import jax.numpy as jnp
        _rk = jax.random.key(seed)
        x = -0.0002928 + 1 * jax.random.normal(jax.random.fold_in(_rk, 1), (16, 256, 256), jnp.float32)
        _lenS = 256 - jax.random.randint(jax.random.fold_in(_rk, 7), (16,), 0, max(1, 256 // 4) + 1, jnp.int32)
        _lenS2 = 256 - jax.random.randint(jax.random.fold_in(_rk, 8), (16,), 0, max(1, 256 // 4) + 1, jnp.int32)
        _ctx_1024P = jax.random.normal(jax.random.fold_in(_rk, 11), (16, 16, 256), jnp.float32)
        _ctx_1024c = jax.random.dirichlet(jax.random.fold_in(_rk, 511), 0.3 * jnp.ones((16,), jnp.float32), (16, 256))
        _ctx_1024t = jnp.einsum('bsk,bkd->bsd', _ctx_1024c, _ctx_1024P)
        _ctx_1024t = _ctx_1024t * jax.lax.rsqrt(jnp.mean(jnp.square(_ctx_1024t)) + 1e-12) * 0.953939
        ctx_1024 = -1.39393e-06 + 0.999914 * (_ctx_1024t + 0.3 * jax.random.normal(jax.random.fold_in(_rk, 611), (16, 256, 256), jnp.float32))
        condB_tau = jax.random.uniform(jax.random.fold_in(_rk, 12), (16,), jnp.float32, 0.0, 1.23395)
        fside_BxS2_0 = -0.00205293 + 0.99739 * jax.random.normal(jax.random.fold_in(_rk, 13), (16, 256), jnp.float32)
        return (x, ctx_1024, condB_tau, fside_BxS2_0)
    x, ctx_1024, condB_tau, fside_BxS2_0 = _rec_inputs()

    def _L0_xcond_setup():
        import jax, jax.numpy as jnp
        import numpy as np
        B, S, D, H = (2, 512, 256, 16)
        DK = D // H

        def _split_heads(x):
            b, s, _ = x.shape
            return x.reshape(b, s, H, DK).transpose(0, 2, 1, 3)
        key = jax.random.key(seed)
        ks = jax.random.split(key, 14)
        inp = {'query': jax.random.normal(ks[0], (B, S, D), jnp.float32), 'key': jax.random.normal(ks[1], (B, S, D), jnp.float32), 'value': jax.random.normal(ks[2], (B, S, D), jnp.float32), 'tau': jax.random.uniform(ks[3], (B, 1), jnp.float32, 0.5, 1.5), 'delta': jax.random.normal(ks[4], (B, S), jnp.float32)}
        sc = 1.0 / np.sqrt(D)
        for i, name in enumerate(['q', 'k', 'v', 'o']):
            inp[f'W{name}'] = jax.random.normal(ks[5 + 2 * i], (D, D), jnp.float32) * sc
            inp[f'b{name}'] = jax.random.normal(ks[6 + 2 * i], (D,), jnp.float32) * 0.01
        return inp
    _L0_xcond_all = _L0_xcond_setup()
    _L0_xcond_in = {k: v for k, v in _L0_xcond_all.items() if k in ('Wq', 'bq', 'Wk', 'bk', 'Wv', 'bv', 'Wo', 'bo')}
    del _L0_xcond_all

    def _L0_ffn_setup():
        import jax, jax.numpy as jnp
        import numpy as np
        import math
        B, T, C = (4, 512, 256)
        E, K = (8, 2)
        EH, SH = (512, 1024)
        CAP_FACTOR = 1.25
        SCALING = 1.0
        FC_MULT = 1.0

        def _capacity(N, k):
            avg = math.ceil(N * k / E)
            return max(int(math.ceil(avg * CAP_FACTOR)), 1)
        key = jax.random.key(seed)
        ks = jax.random.split(key, 6)
        sd = 0.02
        return {'x': jax.random.normal(ks[0], (B, T, C), jnp.float32), 'proj_w': jax.random.normal(ks[1], (E, C), jnp.float32) * sd, 'proj_b': jnp.zeros((E,), jnp.float32), 'expert_bias': jnp.zeros((E,), jnp.float32), 'fc1_w': jax.random.normal(ks[2], (E, EH, C), jnp.float32) * sd, 'fc1_b': jnp.zeros((E, EH), jnp.float32), 'fc2_w': jax.random.normal(ks[3], (E, C, EH), jnp.float32) * sd, 'fc2_b': jnp.zeros((E, C), jnp.float32), 'sh1_w': jax.random.normal(ks[4], (SH, C), jnp.float32) * sd, 'sh1_b': jnp.zeros((SH,), jnp.float32), 'sh2_w': jax.random.normal(ks[5], (C, SH), jnp.float32) * sd, 'sh2_b': jnp.zeros((C,), jnp.float32)}
    _L0_ffn_all = _L0_ffn_setup()
    _L0_ffn_in = {k: v for k, v in _L0_ffn_all.items() if k in ('proj_w', 'proj_b', 'expert_bias', 'fc1_w', 'fc1_b', 'fc2_w', 'fc2_b', 'sh1_w', 'sh1_b', 'sh2_w', 'sh2_b')}
    del _L0_ffn_all
    return {'x': x, 'ctx_1024': ctx_1024, 'condB_tau': condB_tau, 'fside_BxS2_0': fside_BxS2_0, 'L0_xcond_Wq': _L0_xcond_in['Wq'], 'L0_xcond_bq': _L0_xcond_in['bq'], 'L0_xcond_Wk': _L0_xcond_in['Wk'], 'L0_xcond_bk': _L0_xcond_in['bk'], 'L0_xcond_Wv': _L0_xcond_in['Wv'], 'L0_xcond_bv': _L0_xcond_in['bv'], 'L0_xcond_Wo': _L0_xcond_in['Wo'], 'L0_xcond_bo': _L0_xcond_in['bo'], 'L0_ffn_proj_w': _L0_ffn_in['proj_w'], 'L0_ffn_proj_b': _L0_ffn_in['proj_b'], 'L0_ffn_expert_bias': _L0_ffn_in['expert_bias'], 'L0_ffn_fc1_w': _L0_ffn_in['fc1_w'], 'L0_ffn_fc1_b': _L0_ffn_in['fc1_b'], 'L0_ffn_fc2_w': _L0_ffn_in['fc2_w'], 'L0_ffn_fc2_b': _L0_ffn_in['fc2_b'], 'L0_ffn_sh1_w': _L0_ffn_in['sh1_w'], 'L0_ffn_sh1_b': _L0_ffn_in['sh1_b'], 'L0_ffn_sh2_w': _L0_ffn_in['sh2_w'], 'L0_ffn_sh2_b': _L0_ffn_in['sh2_b']}

def reference(x, ctx_1024, condB_tau, fside_BxS2_0, L0_xcond_Wq, L0_xcond_bq, L0_xcond_Wk, L0_xcond_bk, L0_xcond_Wv, L0_xcond_bv, L0_xcond_Wo, L0_xcond_bo, L0_ffn_proj_w, L0_ffn_proj_b, L0_ffn_expert_bias, L0_ffn_fc1_w, L0_ffn_fc1_b, L0_ffn_fc2_w, L0_ffn_fc2_b, L0_ffn_sh1_w, L0_ffn_sh1_b, L0_ffn_sh2_w, L0_ffn_sh2_b):
    import jax
    import jax.numpy as jnp

    def _L0_xcond_ref(query, key, value, tau, delta, Wq, bq, Wk, bk, Wv, bv, Wo, bo):
        import jax, jax.numpy as jnp
        import numpy as np
        B, S, D, H = (2, 512, 256, 16)
        DK = D // H

        def _split_heads(x):
            b, s, _ = x.shape
            return x.reshape(b, s, H, DK).transpose(0, 2, 1, 3)
        q = _split_heads(query @ Wq.T + bq)
        k = _split_heads(key @ Wk.T + bk)
        v = _split_heads(value @ Wv.T + bv)
        scores = jnp.einsum('bhqd,bhkd->bhqk', q, k)
        scores = scores * tau[:, :, None, None] + delta[:, None, None, :]
        scores = scores / jnp.sqrt(jnp.asarray(DK, scores.dtype))
        p_attn = jax.nn.softmax(scores, axis=-1)
        x = jnp.einsum('bhqk,bhkd->bhqd', p_attn, v)
        x = x.transpose(0, 2, 1, 3).reshape(query.shape[0], -1, H * DK)
        return x @ Wo.T + bo

    def _L0_ffn_ref(x, proj_w, proj_b, expert_bias, fc1_w, fc1_b, fc2_w, fc2_b, sh1_w, sh1_b, sh2_w, sh2_b):
        import jax, jax.numpy as jnp
        import numpy as np
        import math
        B, T, C = (4, 512, 256)
        E, K = (8, 2)
        EH, SH = (512, 1024)
        CAP_FACTOR = 1.25
        SCALING = 1.0
        FC_MULT = 1.0

        def _capacity(N, k):
            avg = math.ceil(N * k / E)
            return max(int(math.ceil(avg * CAP_FACTOR)), 1)
        Bx, Tx, Cx = x.shape
        N = Bx * Tx
        xf = x.reshape(N, Cx)
        z = xf @ proj_w.T + proj_b
        s = jax.nn.sigmoid(z) + expert_bias
        logits = jnp.log(jnp.clip(s, 1e-12)) * SCALING
        probs = jax.nn.softmax(logits, axis=-1)
        topk_w, topk_idx = jax.lax.top_k(probs, K)
        topk_w = topk_w / jnp.clip(topk_w.sum(-1, keepdims=True), 1e-12)
        pair_e = topk_idx.reshape(-1)
        pair_w = topk_w.reshape(-1)
        pair_tok = jnp.repeat(jnp.arange(N), K)
        cap = _capacity(N, K)
        assigned = pair_e[None, :] == jnp.arange(E)[:, None]
        wmat = jnp.where(assigned, pair_w[None, :], -jnp.inf)
        kept_w, kept_pair = jax.lax.top_k(wmat, cap)
        valid = kept_w > -jnp.inf
        kept_w = jnp.where(valid, kept_w, 0.0)
        kept_tok = pair_tok[kept_pair]
        xe = xf[kept_tok]
        h = jax.nn.gelu(jnp.einsum('ecd,ehd->ech', xe, fc1_w) + fc1_b[:, None, :], approximate=False)
        oe = jnp.einsum('ech,edh->ecd', h, fc2_w) + fc2_b[:, None, :]
        contrib = oe * kept_w[..., None]
        y = jnp.zeros((N, Cx), x.dtype).at[kept_tok.reshape(-1)].add(contrib.reshape(-1, Cx))
        sh = jax.nn.gelu(xf @ sh1_w.T + sh1_b, approximate=False) @ sh2_w.T + sh2_b
        return ((sh + y) * FC_MULT).reshape(Bx, Tx, Cx)
    x = x + _L0_xcond_ref(_layernorm(x, axis=-1), ctx_1024, ctx_1024, condB_tau[:, None], fside_BxS2_0, L0_xcond_Wq, L0_xcond_bq, L0_xcond_Wk, L0_xcond_bk, L0_xcond_Wv, L0_xcond_bv, L0_xcond_Wo, L0_xcond_bo)
    x = x + _L0_ffn_ref(_layernorm(x, axis=-1), L0_ffn_proj_w, L0_ffn_proj_b, L0_ffn_expert_bias, L0_ffn_fc1_w, L0_ffn_fc1_b, L0_ffn_fc2_w, L0_ffn_fc2_b, L0_ffn_sh1_w, L0_ffn_sh1_b, L0_ffn_sh2_w, L0_ffn_sh2_b)
    return x

_drawn_inputs = setup_inputs


def setup_inputs(seed=0):
    import zlib

    import numpy as np

    out = dict(_drawn_inputs(seed))
    spreads = {'L0_ffn_proj_b': (0.0, 0.1),
     'L0_ffn_expert_bias': (0.0, 0.1),
     'L0_ffn_fc1_b': (0.0, 0.685),
     'L0_ffn_fc2_b': (0.0, 0.1),
     'L0_ffn_sh1_b': (0.0, 0.276),
     'L0_ffn_sh2_b': (0.0, 0.1)}
    factors = {'fside_BxS2_0': 3.594,
     'L0_xcond_bq': 31.519,
     'L0_xcond_bk': 64.0,
     'L0_xcond_bv': 5.219,
     'L0_xcond_bo': 6.252}
    for name, (base, spread) in spreads.items():
        noise = np.random.default_rng([zlib.crc32(name.encode()), seed]).standard_normal(out[name].shape)
        drawn = base * np.exp(spread * noise) if base else spread * noise
        out[name] = jnp.asarray(drawn.astype(out[name].dtype))
    for name, factor in factors.items():
        out[name] = (out[name] * factor).astype(out[name].dtype)
    return out
```

```python
from contextlib import ExitStack

import numpy as np

import concourse.bass as bass
from concourse import mybir

F32 = mybir.dt.float32
F32R = mybir.dt.float32r
BF16 = mybir.dt.bfloat16
U32 = mybir.dt.uint32
ALU = mybir.AluOpType
ACT = mybir.ActivationFunctionType
AX_X = mybir.AxisListType.X

P = 128
B, S, D, H = 16, 256, 256, 16
DK = D // H
EPS = 1e-5
TOK_TILES = S // P
DCH = D // P
NT = B * TOK_TILES
PAIRS = H // 2
HALF = P // 2
GROUP_H = P // DK
QUADS = H // 4
ROW_MAX = 3 * DK
ROW_DELTA = ROW_MAX + 2
STEPS = 11


def consts():
    sel = np.zeros((4, P, PAIRS // 2, P), np.float32)
    parts = {0: (0, 2), 1: (1,), 2: (0, 1), 3: (2,)}
    for n, blocks in parts.items():
        for s in range(PAIRS // 2):
            for par in range(2):
                for blk in blocks:
                    for d in range(DK):
                        sel[n, (2 * s + par) * DK + d, s, par * HALF + blk * DK + d] = 1.0
    rows = np.zeros((P, 2), np.float32)
    for par in range(2):
        rows[par * HALF + ROW_DELTA:par * HALF + ROW_DELTA + 2, 0] = 1.0
        rows[par * HALF + ROW_MAX:par * HALF + ROW_MAX + 2, 1] = 1.0
    return sel.transpose(1, 0, 2, 3).copy(), rows, np.eye(P, dtype=np.float32)


def live(b):
    return not isinstance(b, int) or 0 <= b < B


def pipeline(eng, body):
    for i in (-1, 0, 1):
        body(i, i % 2)
    with eng.Fori(1, B // 2 - 1) as n:
        body(2 * n, 0)
        body(2 * n + 1, 1)
    for i in range(B - 2, B + 2):
        body(i, i % 2)


def attention(nc, ctx0, dram, x_res):
    with ExitStack() as ctx:
        def sb(name, shape, dt=F32):
            return ctx.enter_context(nc.sbuf_tensor(name, shape, dt))

        def psum(name, shape):
            return ctx.enter_context(nc.psum_tensor(name, shape, F32))

        def sem(name):
            return ctx0.enter_context(nc.semaphore(name))

        w_raw = sb("w_raw", [P, 4, DCH, D])
        w_hi = sb("w_hi", [P, 4, DCH, D], F32R)
        w_lo = sb("w_lo", [P, 4, DCH, D], F32R)
        WQ, WK, WV, WO = range(4)
        sel_raw = w_raw[:, :, :, :].rearrange("p a c d -> p (a c d)").rearrange(
            "p (n s m) -> p n s m", n=4, s=PAIRS // 2)
        sel = sb("sel", [P, 4, PAIRS // 2, P], F32R)
        one_rows = sb("one_rows", [P, 2])
        ident = sb("ident", [P, P])
        b_qk = sb("b_qk", [P, 2, DCH])
        bv_row = sb("bv_row", [P, D])
        bo_row = sb("bo_row", [P, D])
        eps_exp = sb("eps_exp", [P, 2, TOK_TILES])
        delta = sb("delta", [B, S])
        delta_hl = sb("delta_hl", [B, 2, S], F32R)
        stats = sb("stats", [P, TOK_TILES, 6])
        mean_var = sb("mean_var", [P, TOK_TILES, 2])
        rstd = sb("rstd", [P, 2, TOK_TILES])
        xn = sb("xn", [P, TOK_TILES, D])
        xnT_hi = sb("xnT_hi", [P, DCH, S], F32R)
        xnT_lo = sb("xnT_lo", [P, DCH, S], F32R)
        ctx_raw = sb("ctx_raw", [P, 2, DCH, S])
        ctx_hi = sb("ctx_hi", [P, 2, DCH, S], F32R)
        ctx_lo = sb("ctx_lo", [P, 2, DCH, S], F32R)
        tau = sb("tau", [P, 2])
        tau_bq = sb("tau_bq", [P, 2, DCH])
        q_f = sb("q_f", [P, 2, S])
        k_f = sb("k_f", [P, 2, S])
        q_hi = sb("q_hi", [P, 2, S], F32R)
        q_lo = sb("q_lo", [P, 2, S], F32R)
        k_hi = sb("k_hi", [P, 2, S], F32R)
        k_lo = sb("k_lo", [P, 2, S], F32R)
        q_st = [sb(f"q_st{n}", [P, PAIRS, S], F32R) for n in range(2)]
        k_st = [sb(f"k_st{n}", [P, H, S], F32R) for n in range(2)]
        row_max = sb("row_max", [P, TOK_TILES, 2, 2, PAIRS // 2])
        max_hi = [sb(f"max_hi{n}", [H // 2, S], F32R) for n in range(2)]
        max_lo = [sb(f"max_lo{n}", [H // 2, S], F32R) for n in range(2)]
        v1 = sb("v1", [P, TOK_TILES, H, 32])
        probs = sb("probs", [P, 8, TOK_TILES, S])
        u = sb("u", [P, QUADS, S])
        recip = sb("recip", [P, TOK_TILES, H])
        o = sb("o", [P, TOK_TILES, D])
        oT_hi = sb("oT_hi", [P, DCH, S], F32R)
        oT_lo = sb("oT_lo", [P, DCH, S], F32R)

        bankA = [psum(f"bankA{n}", [P, 2, S]) for n in range(2)]
        bankM = [psum(f"bankM{n}", [P, 2, S]) for n in range(2)]
        bankS = [psum(f"bankS{n}", [P, 2, S]) for n in range(2)]
        bankV = psum("bankV", [P, 2, S])
        bankD = psum("bankD", [P, 512])

        x_in = [sem("x_in0"), sem("x_in1")]
        w_in = sem("w_in"); sel_in = sem("sel_in"); small_in = sem("small_in"); delta_in = sem("delta_in")
        k_clear = [sem("k_clear0"), sem("k_clear1")]; v_clear = sem("v_clear"); eps_set = sem("eps_set")
        w_split = sem("w_split"); sel_ready = sem("sel_ready"); delta_split = sem("delta_split")
        delta_out = sem("delta_out")
        ctx_in = [sem("ctx_in0"), sem("ctx_in1")]
        delta_rows = [[sem(f"delta_rows{n}{half}") for half in range(2)] for n in range(2)]
        ctx_hi_ready = sem("ctx_hi_ready"); ctx_lo_ready = sem("ctx_lo_ready")
        tau_bq_ready = sem("tau_bq_ready")
        stats_ready = sem("stats_ready"); ln_ready = sem("ln_ready"); var_eps = sem("var_eps")
        rstd_ready = sem("rstd_ready"); xn_ready = sem("xn_ready"); bo_added = sem("bo_added")
        a_filled = sem("a_filled")
        xnT_hi_ready = sem("xnT_hi_ready"); xnT_lo_ready = sem("xnT_lo_ready")
        qk_ready = sem("qk_ready"); qk_hi_ready = sem("qk_hi_ready"); qk_lo_ready = sem("qk_lo_ready")
        q_st_ready = sem("q_st_ready"); k_st_dve = sem("k_st_dve"); k_st_act = sem("k_st_act")
        m_filled = sem("m_filled"); m_free = [sem("m_free0"), sem("m_free1")]
        maxT_filled = sem("maxT_filled"); max_hi_ready = sem("max_hi_ready")
        max_lo_ready = sem("max_lo_ready"); max_rows = [sem("max_rows0"), sem("max_rows1")]
        v_filled = sem("v_filled"); v_ready = sem("v_ready")
        s_filled = sem("s_filled"); exp_done = sem("exp_done")
        pv_done = sem("pv_done"); u_ready = sem("u_ready")
        d_filled = sem("d_filled"); d_free = sem("d_free"); recip_ready = sem("recip_ready")
        oT_hi_ready = sem("oT_hi_ready"); oT_lo_ready = sem("oT_lo_ready")
        x_res_ready = sem("x_res_ready")

        JOB_XNT, JOB_Q, JOB_K = 0, 1, 2
        JOBS = 3 + 2 * QUADS

        def job_qs(m):
            return 3 + 2 * m

        def job_ks(m):
            return 4 + 2 * m

        K_ON_DVE = 2

        def two_loads(b, par):
            return 16 * (b + 2 - par)

        block = ctx.enter_context(nc.Block())

        @block.sync
        def _(sp):
            xv = dram["x"].rearrange("b (c p) d -> p (b c) d", p=P)
            sp.dma_start(x_res[:, 0:4, :], xv[:, 0:4, :]).then_inc(x_in[0], 16)
            sp.dma_start(ident[:, :], dram["ident"]).then_inc(small_in, 16)
            sp.dma_start(one_rows[:, :], dram["one_rows"]).then_inc(small_in, 16)
            sp.dma_start(b_qk[:, :, :], dram["b_qk"]).then_inc(small_in, 16)
            sp.dma_start(bv_row[:, :], dram["bv"].partition_broadcast(P)).then_inc(small_in, 16)
            sp.dma_start(bo_row[:, :], dram["bo"].partition_broadcast(P)).then_inc(small_in, 16)
            sp.dma_start(ctx_raw[:, 0], dram["ctxT"][0].rearrange("(c p) s -> p c s", p=P)).then_inc(ctx_in[0], 16)
            sp.dma_start(tau[:, 0:1], dram["tau"][0:1].partition_broadcast(P)).then_inc(ctx_in[0], 16)
            for n, w in enumerate(("WqT", "WkT", "WvT", "WoT")):
                sp.dma_start(w_raw[:, n], dram[w].rearrange("(c p) d -> p c d", p=P)).then_inc(w_in, 16)
            sp.dma_start(delta[:, :], dram["delta"]).then_inc(delta_in, 16)
            sp.wait_ge(w_split, 2)
            sp.dma_start(sel_raw, dram["sel"]).then_inc(sel_in, 16)
            sp.dma_start(x_res[:, 4:NT, :], xv[:, 4:NT, :]).then_inc(x_in[1], 16)
            sp.wait_ge(delta_split, 2)
            sp.dma_start(dram["delta_hl"], delta_hl[:, :, :].bitcast(F32)).then_inc(delta_out, 16)
            sp.wait_ge(delta_out, 16)

            def load_delta_rows(b, par, half):
                heads = slice(half * H // 2, (half + 1) * H // 2)
                for p in range(2):
                    at = p * HALF + ROW_DELTA
                    dst = k_st[par][at:at + 2, heads, :].rearrange("r (s p) k -> r p s k", p=2)[:, p]
                    src = dram["delta_hl"][bass.ds(b, 1)].rearrange("o r k -> (o r) k")
                    src = src[:, None, :].to_broadcast([2, PAIRS // 2, S])
                    sp.dma_start(dst.bitcast(F32), src).then_inc(delta_rows[par][half], 16)

            def iteration(i, par):
                a, nxt = i + 1, i + 2
                if live(nxt):
                    if live(nxt - 2):
                        sp.wait_ge(qk_lo_ready, 2 * (nxt - 1))
                    sp.dma_start(ctx_raw[:, par], dram["ctxT"][bass.ds(nxt, 1)].rearrange(
                        "o (c p) s -> p (o c) s", p=P)).then_inc(ctx_in[par], 16)
                    sp.dma_start(tau[:, par:par + 1], dram["tau"][bass.ds(nxt, 1)].partition_broadcast(P)).then_inc(ctx_in[par], 16)
                for half in range(2):
                    if live(a):
                        if live(a - 2):
                            sp.wait_ge(s_filled, H * (a - 2) + (half + 1) * H // 2)
                        else:
                            sp.wait_ge(k_clear[1 - par], 1)
                        load_delta_rows(a, 1 - par, half)
                    if live(i):
                        sp.wait_ge(max_hi_ready, 2 * i + half + 1)
                        sp.wait_ge(max_lo_ready, 2 * i + half + 1)
                        for p in range(2):
                            for n, part in enumerate((max_hi[half], max_lo[half])):
                                at = p * HALF + ROW_MAX + n
                                sp.dma_start(q_st[par][at:at + 1, half * PAIRS // 2:(half + 1) * PAIRS // 2, :].bitcast(F32),
                                             part[p * PAIRS // 2:(p + 1) * PAIRS // 2, :].bitcast(F32)).then_inc(max_rows[half], 16)

            pipeline(sp, iteration)

        @block.gpsimd
        def _(pool):
            pool.memset(eps_exp[:, 0], EPS)
            pool.memset(eps_exp[:, 1], -0.5).then_inc(eps_set, 1)
            pool.memset(k_st[0][:, :, :].bitcast(F32), 0.0).then_inc(k_clear[0], 1)
            pool.wait_ge(eps_set, 1)

            def reciprocal_std(b):
                pool.wait_ge(ln_ready, b + 1)
                pool.tensor_tensor(rstd[:, 0], mean_var[:, :, 1], eps_exp[:, 0], ALU.add).then_inc(var_eps, 1)
                pool.wait_ge(var_eps, b + 1)
                pool.tensor_tensor(rstd[:, 1], rstd[:, 0], eps_exp[:, 1], ALU.pow).then_inc(rstd_ready, 1)

            def add_bo(b):
                pool.wait_ge(small_in, 5 * 16)
                pool.wait_ge(xn_ready, b + 1)
                xb = x_res[:, bass.ds(b * TOK_TILES, TOK_TILES), :]
                pool.tensor_tensor(xb, xb, bo_row[:, None, :].to_broadcast([P, TOK_TILES, D]), ALU.add).then_inc(bo_added, 1)

            def iteration(i, par):
                a = i + 1
                if isinstance(i, int) and i == -1:
                    reciprocal_std(0)
                    pool.wait_ge(w_split, 1)
                    pool.tensor_tensor(w_lo[:, :, :, :], w_raw[:, :, :, :], w_hi[:, :, :, :].bitcast(F32), ALU.subtract).then_inc(w_split, 1)
                    iteration_a(a, par)
                    pool.wait_ge(delta_split, 1)
                    pool.tensor_tensor(delta_hl[:, 1], delta[:, :], delta_hl[:, 0].bitcast(F32), ALU.subtract).then_inc(delta_split, 1)
                    pool.memset(k_st[1][:, :, :].bitcast(F32), 0.0).then_inc(k_clear[1], 1)
                    add_bo(0)
                    reciprocal_std(1)
                    pool.memset(v1[:, :, :, :], 0.0).then_inc(v_clear, 1)
                    pool.wait_ge(v_clear, 1)
                    pool.memset(v1[:, :, :, DK:DK + 1], 1.0).then_inc(v_clear, 1)
                    add_bo(1)
                    return
                if live(a):
                    iteration_a(a, par)
                if live(i + 2):
                    reciprocal_std(i + 2)
                    add_bo(i + 2)

            def iteration_a(a, par):
                pool.wait_ge(ctx_in[1 - par], two_loads(a, 1 - par))
                pool.wait_ge(small_in, 5 * 16)
                if live(a - 2):
                    pool.wait_ge(qk_ready, 2 * (a - 1))
                pool.tensor_tensor(tau_bq[:, 1 - par], b_qk[:, 0, :], tau[:, 1 - par:2 - par].to_broadcast([P, DCH]), ALU.mult).then_inc(tau_bq_ready, 1)
                pool.wait_ge(ctx_hi_ready, a + 1)
                pool.tensor_tensor(ctx_lo[:, 1 - par], ctx_raw[:, 1 - par], ctx_hi[:, 1 - par].bitcast(F32), ALU.subtract).then_inc(ctx_lo_ready, 1)
                for n, (f, hi, lo) in enumerate(((q_f, q_hi, q_lo), (k_f, k_hi, k_lo))):
                    pool.wait_ge(qk_hi_ready, 2 * a + n + 1)
                    pool.tensor_tensor(lo[:, :, :], f[:, :, :], hi[:, :, :].bitcast(F32), ALU.subtract).then_inc(qk_lo_ready, 1)

            pipeline(pool, iteration)

        @block.scalar
        def _(act):
            def iteration(i, par):
                a, sm, d = i + 1, i - 1, i - 2
                for t in range(STEPS):
                    if live(sm) and 2 <= t < 2 + PAIRS:
                        for h in (2 * (t - 2), 2 * (t - 2) + 1):
                            act.wait_ge(s_filled, H * sm + h + 1)
                            if h >= 8:
                                act.wait_ge(pv_done, QUADS * sm + (h - 8) // 4 + 1)
                            elif live(sm - 1):
                                act.wait_ge(pv_done, QUADS * (sm - 1) + (h + 8) // 4 + 1)
                            act.activation(probs[:, h % 8], bankS[h % 2][:, :, :], ACT.Exp, scale=float(DK) ** -0.5).then_inc(exp_done, 1)
                    if live(a):
                        if t == 0:
                            act.wait_ge(a_filled, JOBS * a + JOB_XNT + 1)
                            if live(a - 1):
                                act.wait_ge(a_filled, JOBS * (a - 1) + JOB_Q + 1)
                            act.activation(xnT_hi[:, :, :], bankA[0][:, :, :], ACT.Identity).then_inc(xnT_hi_ready, 1)
                        if t == 1:
                            act.wait_ge(a_filled, JOBS * a + JOB_Q + 1)
                            act.wait_ge(tau_bq_ready, a + 1)
                            if live(a - 1):
                                act.wait_ge(qk_lo_ready, 2 * (a - 1) + 1)
                            for g in range(2):
                                ins = act.activation(q_f[:, g], bankA[1][:, g], ACT.Identity, bias=tau_bq[:, 1 - par, g:g + 1], scale=tau[:, 1 - par:2 - par])
                            ins.then_inc(qk_ready, 1)
                        if t == 2:
                            act.wait_ge(a_filled, JOBS * a + JOB_K + 1)
                            if live(a - 1):
                                act.wait_ge(qk_lo_ready, 2 * (a - 1) + 2)
                            for g in range(2):
                                ins = act.activation(k_f[:, g], bankA[0][:, g], ACT.Identity, bias=b_qk[:, 1, g:g + 1])
                            ins.then_inc(qk_ready, 1)
                        if t >= 4 and t % 2 == 0:
                            m = (t - 4) // 2
                            act.wait_ge(a_filled, JOBS * a + job_qs(m) + 1)
                            if live(a - 2):
                                act.wait_ge(s_filled, H * (a - 2) + 4 * (m + 1))
                            act.activation(q_st[1 - par][:, 2 * m:2 * m + 2], bankA[job_qs(m) % 2][:, :, :], ACT.Identity, bias=one_rows[:, 0:1]).then_inc(q_st_ready, 1)
                            if m >= K_ON_DVE:
                                act.wait_ge(a_filled, JOBS * a + job_ks(m) + 1)
                                if not live(a - 2):
                                    act.wait_ge(k_clear[1 - par], 1)
                                for p in range(2):
                                    rows = slice(p * HALF, p * HALF + ROW_DELTA)
                                    ins = act.activation(k_st[1 - par][rows, 4 * m:4 * m + 4].rearrange("r (s p) k -> r p s k", p=2)[:, p],
                                                         bankA[job_ks(m) % 2][rows], ACT.Identity, bias=one_rows[rows, 1:2])
                                ins.then_inc(k_st_act, 1)
                    if live(d) and t == 5:
                        act.wait_ge(d_filled, 4 * d + 3)
                        if live(d - 1):
                            act.wait_ge(d_filled, 4 * (d - 1) + 4)
                        act.activation(oT_hi[:, :, :].rearrange("p c s -> p (c s)"), bankD[:, :], ACT.Identity).then_inc(oT_hi_ready, 1)
                    if live(sm) and t in (6, 10):
                        half = (t - 6) // 4
                        act.wait_ge(pv_done, QUADS * sm + 2 * half + 2)
                        if live(sm - 1):
                            act.wait_ge(d_filled, 4 * (sm - 1) + 2)
                        act.activation(u[:, 2 * half:2 * half + 2], bankV[:, :, :], ACT.Identity).then_inc(u_ready, 1)
                    if live(i) and t in (6, 9):
                        half = t // 9
                        act.wait_ge(maxT_filled, 2 * i + half + 1)
                        if live(i - 1):
                            act.wait_ge(max_rows[half], 64 * i)
                        act.activation(max_hi[half][:, :], bankD[0:H // 2, 0:S], ACT.Identity, scale=-1.0).then_inc(max_hi_ready, 1)

            act.wait_ge(small_in, 5 * 16)
            pipeline(act, iteration)

        @block.vector
        def _(dve):
            dve.wait_ge(w_in, 64)
            dve.tensor_copy(w_hi[:, :, :, :], w_raw[:, :, :, :]).then_inc(w_split, 1)
            dve.wait_ge(delta_in, 16)
            dve.tensor_copy(delta_hl[:, 0], delta[:, :]).then_inc(delta_split, 1)

            def statistics(b):
                for c in range(TOK_TILES):
                    ins = dve.bn_stats(stats[:, c], x_res[:, bass.ds(b * TOK_TILES + c, 1), :].rearrange("p o d -> p (o d)"))
                ins.then_inc(stats_ready, 1)

            def mean_variance(b):
                for c in range(TOK_TILES):
                    ins = dve.bn_aggr(mean_var[:, c], stats[:, c])
                ins.then_inc(ln_ready, 1)

            def normalise(b):
                dve.wait_ge(rstd_ready, b + 1)
                if live(b - 1):
                    dve.wait_ge(a_filled, JOBS * (b - 1) + JOB_XNT + 1)
                for c in range(TOK_TILES):
                    ins = dve.tensor_scalar(xn[:, c], x_res[:, bass.ds(b * TOK_TILES + c, 1), :].rearrange("p o d -> p (o d)"),
                                            mean_var[:, c, 0:1], rstd[:, 1, c:c + 1], ALU.subtract, ALU.mult)
                ins.then_inc(xn_ready, 1)

            def iteration(i, par):
                a, d = i + 1, i - 2
                if isinstance(i, int) and i == -1:
                    dve.wait_ge(x_in[0], 16)
                    statistics(0)
                    dve.wait_ge(stats_ready, 1)
                    mean_variance(0)
                    normalise(0)
                for t in range(STEPS):
                    if live(a):
                        if t == 0:
                            dve.wait_ge(ctx_in[1 - par], two_loads(a, 1 - par))
                            if live(a - 2):
                                dve.wait_ge(v_filled, a - 1)
                            dve.tensor_copy(ctx_hi[:, 1 - par], ctx_raw[:, 1 - par]).then_inc(ctx_hi_ready, 1)
                            dve.wait_ge(xnT_hi_ready, a + 1)
                            dve.tensor_tensor(xnT_lo[:, :, :], bankA[0][:, :, :], xnT_hi[:, :, :].bitcast(F32), ALU.subtract).then_inc(xnT_lo_ready, 1)
                        if t in (2, 3):
                            n = t - 2
                            f, hi = ((q_f, q_hi), (k_f, k_hi))[n]
                            dve.wait_ge(qk_ready, 2 * a + n + 1)
                            if live(a - 1):
                                dve.wait_ge(a_filled, JOBS * a)
                            dve.tensor_copy(hi[:, :, :], f[:, :, :]).then_inc(qk_hi_ready, 1)
                        if t == 3 and isinstance(i, int) and i == -1:
                            dve.wait_ge(sel_in, 16)
                            dve.tensor_copy(sel[:, :, :, :], sel_raw).then_inc(sel_ready, 1)
                        if t >= 4 and t % 2 == 0 and (t - 4) // 2 < K_ON_DVE:
                            m = (t - 4) // 2
                            dve.wait_ge(a_filled, JOBS * a + job_ks(m) + 1)
                            if live(a - 2):
                                dve.wait_ge(s_filled, H * (a - 2) + 4 * (m + 1))
                            else:
                                dve.wait_ge(k_clear[1 - par], 1)
                            for p in range(2):
                                rows = slice(p * HALF, p * HALF + ROW_DELTA)
                                ins = dve.tensor_scalar(k_st[1 - par][rows, 4 * m:4 * m + 4].rearrange("r (s p) k -> r p s k", p=2)[:, p],
                                                        bankA[job_ks(m) % 2][rows], one_rows[rows, 1:2], None, ALU.add)
                            ins.then_inc(k_st_dve, 1)
                    if live(i) and t < PAIRS:
                        if t == 0 and live(i - 1):
                            dve.wait_ge(maxT_filled, 2 * i)
                        if t == 6 and live(i + 2):
                            dve.wait_ge(stats_ready, i + 3)
                        for c in range(TOK_TILES):
                            dve.wait_ge(m_filled, 2 * PAIRS * i + 2 * t + c + 1)
                            dve.tensor_reduce(row_max[:, c, t // (PAIRS // 2), :, t % (PAIRS // 2)], bankM[c][:, :, :], AX_X, ALU.max).then_inc(m_free[c], 1)
                    if live(i + 2):
                        if t == 5:
                            if isinstance(i, int) and i == 0:
                                dve.wait_ge(x_in[1], 16)
                            statistics(i + 2)
                        if t == 6:
                            if isinstance(i, int) and i == -1:
                                dve.wait_ge(stats_ready, i + 3)
                            mean_variance(i + 2)
                        if t == 7:
                            normalise(i + 2)
                    if live(d) and t in (1, 3):
                        c = t // 2
                        dve.wait_ge(d_filled, 4 * d + c + 1)
                        turned = bankD[:, :].rearrange("p (h k) -> p h k", h=H)
                        dve.reciprocal(recip[:, c], turned[:, :, DK]).then_inc(recip_ready, 1)
                        dve.wait_ge(recip_ready, 2 * d + c + 1)
                        dve.tensor_tensor(o[:, c].rearrange("p (h k) -> p h k", h=H), turned[:, :, 0:DK],
                                          recip[:, c, :, None].to_broadcast([P, H, DK]), ALU.mult).then_inc(d_free, 1)
                    if live(d) and t == 5:
                        dve.wait_ge(oT_hi_ready, d + 1)
                        dve.tensor_tensor(oT_lo[:, :, :].rearrange("p c s -> p (c s)"), bankD[:, :],
                                          oT_hi[:, :, :].rearrange("p c s -> p (c s)").bitcast(F32), ALU.subtract).then_inc(d_free, 1)
                    if live(d) and t == 7:
                        dve.wait_ge(d_filled, 4 * d + 4)
                        dve.wait_ge(bo_added, d + 1)
                        xb = x_res[:, bass.ds(d * TOK_TILES, TOK_TILES), :].rearrange("p c d -> p (c d)")
                        dve.tensor_tensor(xb, bankD[:, :], xb, ALU.add).then_inc(d_free, 1)
                    if live(i) and t in (6, 9):
                        half = t // 9
                        dve.wait_ge(max_hi_ready, 2 * i + half + 1)
                        if live(i - 1):
                            dve.wait_ge(max_rows[half], 64 * i)
                        dve.scalar_tensor_tensor(out=max_lo[half][:, :], in0=bankD[0:H // 2, 0:S], scalar=-1.0,
                                                 in1=max_hi[half][:, :].bitcast(F32), op0=ALU.mult, op1=ALU.subtract).then_inc(max_lo_ready, 1)
                    if live(i) and t == 10:
                        dve.wait_ge(v_filled, i + 1)
                        if live(i - 1):
                            dve.wait_ge(pv_done, QUADS * i)
                        else:
                            dve.wait_ge(v_clear, 2)
                        dve.tensor_tensor(v1[:, :, :, 0:DK], bankM[1][:, :, :].rearrange("p c (h k) -> p c h k", h=H),
                                          bv_row[:, None, :].to_broadcast([P, TOK_TILES, D]).rearrange("p c (h k) -> p c h k", h=H), ALU.add).then_inc(v_ready, 1)

            dve.wait_ge(small_in, 5 * 16)
            pipeline(dve, iteration)

        @block.tensor
        def _(pe):
            def three(out, terms):
                n = len(terms) * 3
                k = 0
                for (lh, ll), (rh, rl) in terms:
                    for lhs, rhs in ((lh, rh), (lh, rl), (ll, rh)):
                        ins = pe.matmul(out, lhs, rhs, start=(k == 0), stop=(k == n - 1))
                        k += 1
                return ins

            def project(bank, w, hi, lo):
                for g in range(DCH):
                    cols = slice(g * P, (g + 1) * P)
                    ins = three(bank[:, g], [((w_hi[:, w, c, cols], w_lo[:, w, c, cols]), (hi[:, c], lo[:, c])) for c in range(DCH)])
                return ins

            def stack(bank, m, which, hi, lo):
                for s in range(2):
                    pair = 2 * m + s
                    g, local = pair // (PAIRS // 2), pair % (PAIRS // 2)
                    pe.matmul(bank[:, s], sel[:, 2 * which, local], hi[:, g], start=True, stop=False)
                    ins = pe.matmul(bank[:, s], sel[:, 2 * which + 1, local], lo[:, g], start=False, stop=True)
                return ins

            def turn_maxima(i, half):
                for c in range(TOK_TILES):
                    pe.wait_ge(m_free[c], PAIRS * i + (half + 1) * PAIRS // 2)
                if live(i - 2):
                    pe.wait_ge(d_free, 4 * (i - 2) + 3 + half)
                if half == 1:
                    pe.wait_ge(max_lo_ready, 2 * i + 1)
                elif live(i - 1):
                    pe.wait_ge(max_lo_ready, 2 * i)
                for c in range(TOK_TILES):
                    ins = pe.transpose(bankD[0:H // 2, c * P:(c + 1) * P], row_max[:, c, half].rearrange("p a b -> p (a b)"), ident[:, :])
                ins.then_inc(maxT_filled, 1)

            def iteration(i, par):
                a, sm, d = i + 1, i - 1, i - 2
                for t in range(STEPS):
                    if live(sm) and 2 <= t < 2 + PAIRS:
                        if t in (2, 6):
                            pe.wait_ge(max_rows[t // 6], 64 * (sm + 1))
                        for h in (2 * (t - 2), 2 * (t - 2) + 1):
                            if h >= 2:
                                pe.wait_ge(exp_done, H * sm + h - 1)
                            elif live(sm - 1):
                                pe.wait_ge(exp_done, H * sm + h - 1)
                            for c in range(TOK_TILES):
                                ins = pe.matmul(bankS[h % 2][:, c], k_st[1 - par][:, h, c * P:(c + 1) * P], q_st[1 - par][:, h // 2], start=True, stop=True)
                            ins.then_inc(s_filled, 1)
                    if live(a):
                        if t == 0:
                            pe.wait_ge(xn_ready, a + 1)
                            if live(a - 1):
                                pe.wait_ge(k_st_act, 2 * a)
                            for c in range(DCH):
                                for tt in range(TOK_TILES):
                                    ins = pe.transpose(bankA[0][:, c, tt * P:(tt + 1) * P], xn[:, tt, c * P:(c + 1) * P], ident[:, :])
                            ins.then_inc(a_filled, 1)
                        if t == 1:
                            pe.wait_ge(xnT_lo_ready, a + 1)
                            pe.wait_ge(w_split, 2)
                            if live(a - 1):
                                pe.wait_ge(q_st_ready, QUADS * a)
                            project(bankA[1], WQ, xnT_hi, xnT_lo).then_inc(a_filled, 1)
                        if t == 2:
                            pe.wait_ge(ctx_hi_ready, a + 1)
                            pe.wait_ge(ctx_lo_ready, a + 1)
                            project(bankA[0], WK, ctx_hi[:, 1 - par], ctx_lo[:, 1 - par]).then_inc(a_filled, 1)
                        if t >= 4 and t % 2 == 0:
                            m = (t - 4) // 2
                            if m == 0:
                                pe.wait_ge(qk_lo_ready, 2 * a + 1)
                                pe.wait_ge(qk_ready, 2 * a + 1)
                                pe.wait_ge(sel_ready, 1)
                            else:
                                pe.wait_ge(q_st_ready, QUADS * a + m)
                            stack(bankA[1], m, 0, q_hi, q_lo).then_inc(a_filled, 1)
                            if m == 0:
                                pe.wait_ge(qk_lo_ready, 2 * a + 2)
                                pe.wait_ge(qk_ready, 2 * a + 2)
                            elif m <= K_ON_DVE:
                                pe.wait_ge(k_st_dve, K_ON_DVE * a + m)
                            else:
                                pe.wait_ge(k_st_act, (QUADS - K_ON_DVE) * a + m - K_ON_DVE)
                            stack(bankA[0], m, 1, k_hi, k_lo).then_inc(a_filled, 1)
                    if live(i) and t < PAIRS:
                        if t % 2 == 0:
                            m = t // 2
                            pe.wait_ge(q_st_ready, QUADS * i + m + 1)
                            if m < K_ON_DVE:
                                pe.wait_ge(k_st_dve, K_ON_DVE * i + m + 1)
                            else:
                                pe.wait_ge(k_st_act, (QUADS - K_ON_DVE) * i + m - K_ON_DVE + 1)
                        if t % 4 == 0:
                            pe.wait_ge(delta_rows[par][t // 4], two_loads(i, par))
                        for c in range(TOK_TILES):
                            if t > 0:
                                pe.wait_ge(m_free[c], PAIRS * i + t)
                            elif live(i - 1):
                                pe.wait_ge((m_free[0], v_ready)[c], (PAIRS * i, i)[c])
                            for p in range(2):
                                ins = pe.matmul(bankM[c][:, p], q_st[par][:, t, c * P:(c + 1) * P], k_st[par][:, 2 * t + p], start=True, stop=True)
                            ins.then_inc(m_filled, 1)
                    if live(d) and t in (1, 3):
                        c = t // 2
                        if c == 0:
                            pe.wait_ge(u_ready, 2 * (d + 1))
                        if c == 1:
                            pe.wait_ge(d_free, 4 * d + 1)
                        elif live(i - 1):
                            pe.wait_ge(max_lo_ready, 2 * i)
                        else:
                            pe.wait_ge(d_free, 4 * d)
                        for g in range(QUADS):
                            ins = pe.transpose(bankD[:, g * P:(g + 1) * P], u[:, g, c * P:(c + 1) * P], ident[:, :])
                        ins.then_inc(d_filled, 1)
                    if live(d) and t == 5:
                        pe.wait_ge(d_free, 4 * d + 2)
                        for g in range(DCH):
                            for c in range(TOK_TILES):
                                ins = pe.transpose(bankD[:, g * S + c * P:g * S + (c + 1) * P], o[:, c, g * P:(g + 1) * P], ident[:, :])
                        ins.then_inc(d_filled, 1)
                    if live(i) and t == 6:
                        turn_maxima(i, 0)
                    if live(d) and t == 7:
                        pe.wait_ge(d_free, 4 * d + 3)
                        if live(i):
                            pe.wait_ge(max_lo_ready, 2 * i + 1)
                        for c in range(TOK_TILES):
                            cols = slice(c * P, (c + 1) * P)
                            ins = three(bankD[:, c * D:(c + 1) * D], [((oT_hi[:, g, cols], oT_lo[:, g, cols]), (w_hi[:, WO, g], w_lo[:, WO, g])) for g in range(DCH)])
                        ins.then_inc(d_filled, 1)
                    if live(sm) and t >= 4 and t % 2 == 0:
                        g = (t - 4) // 2
                        pe.wait_ge(exp_done, H * sm + 4 * (g + 1))
                        if g == 0:
                            pe.wait_ge(v_ready, sm + 1)
                        if g == 2:
                            pe.wait_ge(u_ready, 2 * sm + 1)
                        elif g == 0 and live(sm - 1):
                            pe.wait_ge(u_ready, 2 * sm)
                        for c in range(TOK_TILES):
                            for j in range(4):
                                h = 4 * g + j
                                ins = pe.matmul(bankV[32 * j:32 * j + 32, g % 2], v1[:, c, h], probs[:, h % 8, c], start=(c == 0), stop=(c == TOK_TILES - 1),
                                                skip_group_check=True)
                        ins.then_inc(pv_done, 1)
                    if live(i) and t == 9:
                        turn_maxima(i, 1)
                    if live(i) and t == 10:
                        for c in range(TOK_TILES):
                            cols = slice(c * P, (c + 1) * P)
                            ins = three(bankM[1][:, c], [((ctx_hi[:, par, g, cols], ctx_lo[:, par, g, cols]), (w_hi[:, WV, g], w_lo[:, WV, g])) for g in range(DCH)])
                        ins.then_inc(v_filled, 1)

            pe.wait_ge(small_in, 5 * 16)
            pipeline(pe, iteration)


E_N, EH, SH = 8, 512, 1024
CAP = 1280
N_TOK = B * S
SUPER = 4
NS = NT // SUPER
ROW = D + 4
COL_W0, COL_W1, COL_TOK, COL_E0 = D, D + 1, D + 2, D + 3
BITS = 30
FAR = 1 << 14


def route_consts():
    p = np.arange(P)
    tri = (p[:, None] < p[None, :]).astype(np.float32)
    experts = np.zeros((P, 3, E_N), np.float32)
    experts[:, 0] = np.arange(E_N)
    experts[:, 1] = E_N - np.arange(E_N)
    experts[:, 2] = CAP * np.arange(E_N)
    token = (np.arange(NT)[None, :] * P + p[:, None] + 1).astype(np.float32)
    return tri, experts, token


def route_and_shared(nc, ctx0, dram, x_res):
    with ExitStack() as ctx:
        def sb(name, shape, dt=F32):
            return ctx.enter_context(nc.sbuf_tensor(name, shape, dt))

        def psum(name, shape, dt=F32):
            return ctx.enter_context(nc.psum_tensor(name, shape, dt))

        def sem(name):
            return ctx0.enter_context(nc.semaphore(name))

        rows = sb("rows", [P, NT, ROW])
        xT_hi = sb("xT_hi", [P, DCH, N_TOK], F32R)
        xT_lo = sb("xT_lo", [P, DCH, N_TOK], F32R)
        JC = SH // P
        w1_hi = sb("sh1_hi", [P, DCH, SH], F32R)
        w1_lo = sb("sh1_lo", [P, DCH, SH], F32R)
        w2_hi = sb("sh2_hi", [P, JC, D], F32R)
        w2_lo = sb("sh2_lo", [P, JC, D], F32R)
        b1 = sb("sh1_b", [P, JC])
        b2_row = sb("sh2_b", [P, D])
        pw_raw = sb("pw_raw", [P, DCH, E_N])
        pw_hi = sb("pw_hi", [P, DCH, P], F32R)
        pw_lo = sb("pw_lo", [P, DCH, P], F32R)
        pb_eb = sb("pb_eb", [P, 2, E_N])
        ident = sb("ident2", [P, P])
        tri_f = sb("tri_f", [P, P])
        tri = sb("tri", [P, P], BF16)
        ones = sb("ones", [P, P], BF16)
        experts = sb("experts", [P, 3, E_N])
        token = sb("token", [P, NT])
        eps_exp = sb("eps_exp2", [P, 2, NT])
        xs = [sb(f"xs{n}", [P, SUPER, D]) for n in range(2)]
        z_turn = sb("z_turn", [P, SUPER * P])
        h_f = [sb(f"h_f{n}", [P, SUPER * P]) for n in range(2)]
        h_hi = [sb(f"h_hi{n}", [P, SUPER * P], F32R) for n in range(2)]
        h_lo = [sb(f"h_lo{n}", [P, SUPER * P], F32R) for n in range(2)]
        zero_row = sb("zero_row", [P, ROW])
        w_stage = sb("w_stage", [P, DCH * SH // 2])

        bank_t = [psum(f"bank_t{n}", [P, DCH, 2 * P]) for n in range(2)]
        bank_z = psum("bank_z", [P, SUPER * P])
        bank_r = psum("bank_r", [P, SUPER, P])
        acc = [psum(f"acc{n}", [P, D]) for n in range(SUPER)]
        bank_h = bank_t

        mu = sb("mu", [P, NT]); var = sb("var", [P, NT]); dif = sb("dif", [P, NT])
        rstd = sb("rstd2", [P, NT])
        stats = sb("stats2", [P, NT, 6])

        def grid(name, dt=F32):
            return sb(name, [P, E_N, NT], dt)

        z = grid("z"); prob = grid("prob"); g0 = grid("g0"); g1 = grid("g1")
        first = grid("first"); second = grid("second"); w_mask = grid("w_mask"); kept = grid("kept")
        marks = grid("marks", BF16)
        per_tok = sb("per_tok", [P, 6, NT])
        slot_f = sb("slot_f", [P, NT])
        slot = sb("slot", [P, 2, NT], U32)
        bound = sb("bound", [P, E_N], U32)
        cand = sb("cand", [P, E_N], U32)
        bit = sb("bit", [P, E_N], U32)
        over = sb("over", [P, E_N], U32)
        count = sb("count", [P, E_N], BF16)
        room = sb("room", [P, E_N])

        small_in = sem("f_small"); w_in = sem("f_w_in"); w_staged = sem("f_w_staged"); w_done = sem("f_w_done")
        const = sem("f_const"); chain = sem("f_chain"); pool_ln = sem("f_pool_ln"); rstd_ready = sem("f_rstd")
        xs_ready = sem("f_xs"); rows_copied = sem("f_rows_copied"); t_filled = sem("f_t_filled")
        xT_hi_ready = sem("f_xT_hi"); xT_ready = sem("f_xT"); z_filled = sem("f_z_filled"); z_copied = sem("f_z_copied")
        zr_filled = sem("f_zr_filled"); z_ready = sem("f_z_ready")
        sig_in = sem("f_sig_in"); sig_done = sem("f_sig")
        search = sem("f_search"); counted = sem("f_counted"); cnt_ready = sem("f_cnt")
        marked = sem("f_marked"); summed = sem("f_summed"); slots_ready = sem("f_slots"); rows_ready = sem("f_rows")
        sent = sem("f_sent"); zeroed = sem("f_zeroed")
        h_filled = sem("f_h_filled"); h_act = sem("f_h_act"); h_high = sem("f_h_high"); h_ready = sem("f_h_ready")
        acc_filled = sem("f_acc"); acc_free = sem("f_acc_free"); out_sem = sem("f_out")
        y_done = sem("f_y"); act_past = sem("f_act_past")

        block = ctx.enter_context(nc.Block())
        pieces = [(w1_hi, w1_lo, "sh1T", c) for c in range(2)] + [(w2_hi, w2_lo, "sh2T", c) for c in range(2)]

        def piece(t, c):
            return t[:, :, :].rearrange("p a b -> p (a b)")[:, c * SH:(c + 1) * SH]

        @block.sync
        def _(sp):
            for name, dst in (("pw", pw_raw), ("pb_eb", pb_eb), ("experts", experts)):
                sp.dma_start(dst[:, :, :], dram[name]).then_inc(small_in, 16)
            for name, dst in (("ident", ident), ("tri", tri_f), ("token", token), ("sh1_b", b1)):
                sp.dma_start(dst[:, :], dram[name]).then_inc(small_in, 16)
            sp.dma_start(b2_row[:, :], dram["sh2_b"].partition_broadcast(P)).then_inc(small_in, 16)
            sp.wait_ge(const, 5)
            sp.dma_start(dram["slots"].rearrange("(p n) r -> p n r", p=P), zero_row[:, None, :].to_broadcast([P, E_N * CAP // P, ROW])).then_inc(zeroed, 16)
            for n, (hi, lo, name, c) in enumerate(pieces):
                if n:
                    sp.wait_ge(w_done, n)
                sp.dma_start(w_stage[:, :], dram[name][:, c * SH:(c + 1) * SH]).then_inc(w_staged, 16)
            sp.wait_ge(acc_free, SUPER * NS)
            sp.dma_start(dram["out"].rearrange("b (c p) d -> p (b c) d", p=P), x_res[:, :, :]).then_inc(out_sem, 16)
            sp.wait_ge(out_sem, 16)

        @block.gpsimd
        def _(pool):
            pool.memset(eps_exp[:, 0], EPS)
            pool.memset(eps_exp[:, 1], -0.5).then_inc(const, 1)
            pool.memset(pw_hi[:, :, :].bitcast(F32), 0.0).then_inc(const, 1)
            pool.memset(pw_lo[:, :, :].bitcast(F32), 0.0).then_inc(const, 1)
            pool.memset(ones[:, :], 1.0).then_inc(const, 1)
            pool.memset(zero_row[:, :], 0.0).then_inc(const, 1)
            pool.sem_inc(rows_copied, 1)
            pool.wait_ge(const, 5)
            pool.wait_ge(pool_ln, 1)
            pool.tensor_tensor(var[:, :], var[:, :], eps_exp[:, 0], ALU.add).then_inc(pool_ln, 1)
            pool.wait_ge(pool_ln, 2)
            pool.tensor_tensor(rstd[:, :], var[:, :], eps_exp[:, 1], ALU.pow).then_inc(rstd_ready, 1)

            def keep_rows(s, n):
                pool.wait_ge(xs_ready, s + 1)
                pool.tensor_copy(rows[:, bass.ds(s * SUPER, SUPER), 0:D], xs[n][:, :, :]).then_inc(rows_copied, 1)

            with pool.Fori(0, NS // 2) as k:
                keep_rows(2 * k, 0)
                keep_rows(2 * k + 1, 1)
            pool.wait_ge(rows_ready, 1)
            pool.wait_ge(slots_ready, 2)
            pool.wait_ge(zeroed, 16)
            for t in range(NT):
                for k in range(2):
                    pool.indirect_dma_start(out=dram["slots"], out_offset=bass.IndirectOffsetOnAxis(ap=slot[:, k, t:t + 1], axis=0),
                                            in_=rows[:, t, :], in_offset=None, bounds_check=E_N * CAP - 1, oob_is_err=False).then_inc(sent, 16)
            pool.wait_ge(sent, 16 * 2 * NT)

        @block.scalar
        def _(act):
            def high(s, half):
                act.wait_ge(t_filled, 2 * s + half + 1)
                act.sem_inc(act_past, 1)
                act.activation(xT_hi[:, :, bass.ds(s * SUPER * P + half * 2 * P, 2 * P)], bank_t[half][:, :, :], ACT.Identity).then_inc(xT_hi_ready, 1)

            with act.Fori(0, NS) as s:
                high(s, 0)
                high(s, 1)
            act.wait_ge(sig_in, 1)
            act.activation(z[:, :, :], z[:, :, :], ACT.Sigmoid).then_inc(sig_done, 1)
            act.wait_ge(small_in, 8 * 16)

            def hidden(s):
                for j in range(JC):
                    n = j % 2
                    act.wait_ge(h_filled, s * JC + j + 1)
                    if j >= 2:
                        act.wait_ge(h_ready, s * JC + j - 1)
                    act.activation(h_f[n][:, :], bank_h[n][:, :, :].rearrange("p a b -> p (a b)"), ACT.Gelu, bias=b1[:, j:j + 1]).then_inc(h_act, 1)

            with act.Fori(0, NS) as s:
                hidden(s)

        @block.vector
        def _(dve):
            links = [0]

            def link(ins):
                links[0] += 1
                ins.then_inc(chain, 1)
                dve.wait_ge(chain, links[0])

            dve.wait_ge(small_in, 8 * 16)
            dve.wait_ge(const, 5)
            dve.tensor_copy(tri[:, :], tri_f[:, :])
            link(dve.tensor_copy(pw_hi[:, :, 0:E_N], pw_raw[:, :, :]))
            link(dve.tensor_tensor(pw_lo[:, :, 0:E_N], pw_raw[:, :, :], pw_hi[:, :, 0:E_N].bitcast(F32), ALU.subtract))
            for t in range(NT):
                ins = dve.bn_stats(stats[:, t], x_res[:, t, :])
            link(ins)
            even, odd = stats[:, :, 1], stats[:, :, 4]
            dve.tensor_tensor(mu[:, :], even, odd, ALU.add)
            link(dve.tensor_tensor(dif[:, :], even, odd, ALU.subtract))
            dve.tensor_tensor(var[:, :], stats[:, :, 2], stats[:, :, 5], ALU.add)
            dve.tensor_scalar(mu[:, :], mu[:, :], 0.5, None, ALU.mult)
            link(dve.scalar_tensor_tensor(out=dif[:, :], in0=dif[:, :], scalar=0.25, in1=dif[:, :], op0=ALU.mult, op1=ALU.mult))
            dve.scalar_tensor_tensor(out=var[:, :], in0=var[:, :], scalar=1.0 / D, in1=dif[:, :], op0=ALU.mult, op1=ALU.add).then_inc(pool_ln, 1)
            dve.wait_ge(rstd_ready, 1)

            def layernorm(s, n):
                dve.wait_ge(rows_copied, s + 1)
                for j in range(SUPER):
                    t = s * SUPER + j
                    ins = dve.tensor_scalar(xs[n][:, j], x_res[:, bass.ds(t, 1), :].rearrange("p o d -> p (o d)"),
                                            mu[:, bass.ds(t, 1)], rstd[:, bass.ds(t, 1)], ALU.subtract, ALU.mult)
                ins.then_inc(xs_ready, 1)

            def low(s):
                for half in range(2):
                    dve.wait_ge(xT_hi_ready, 2 * s + half + 1)
                    at = bass.ds(s * SUPER * P + half * 2 * P, 2 * P)
                    dve.tensor_tensor(xT_lo[:, :, at], bank_t[half][:, :, :], xT_hi[:, :, at].bitcast(F32), ALU.subtract).then_inc(xT_ready, 1)
                dve.wait_ge(z_filled, s + 1)
                dve.tensor_copy(z_turn[:, :], bank_z[:, :]).then_inc(z_copied, 1)
                dve.wait_ge(zr_filled, s + 1)
                dve.tensor_tensor(z[:, :, bass.ds(s * SUPER, SUPER)], bank_r[:, :, 0:E_N].rearrange("p t e -> p e t"),
                                  pb_eb[:, 0, :, None].to_broadcast([P, E_N, SUPER]), ALU.add).then_inc(z_ready, 1)

            with dve.Fori(0, NS // 2) as k:
                layernorm(2 * k, 0)
                low(2 * k)
                layernorm(2 * k + 1, 1)
                low(2 * k + 1)

            for n, (hi, lo, name, c) in enumerate(pieces):
                dve.wait_ge(w_staged, 16 * (n + 1))
                link(dve.tensor_copy(piece(hi, c), w_stage[:, :]))
                dve.tensor_tensor(piece(lo, c), w_stage[:, :], piece(hi, c).bitcast(F32), ALU.subtract).then_inc(w_done, 1)

            dve.wait_ge(z_ready, NS)
            dve.tensor_copy(g0[:, :, 0:1], z[:, :, 0:1]).then_inc(sig_in, 1)
            dve.wait_ge(sig_done, 1)

            def over_experts(t):
                return t[:, :, :].rearrange("p e t -> p t e")

            def each_token(t):
                return t[:, None, :].to_broadcast([P, E_N, NT])

            def each_expert(t):
                return t[:, :, None].to_broadcast([P, E_N, NT])

            best, norm, p0, p1, w0, w1 = (per_tok[:, n] for n in range(6))
            link(dve.tensor_tensor(z[:, :, :], z[:, :, :], each_expert(pb_eb[:, 1]), ALU.add))
            link(dve.tensor_scalar(z[:, :, :], z[:, :, :], 1e-12, None, ALU.max))
            link(dve.tensor_reduce(best, over_experts(z), AX_X, ALU.max))
            link(dve.reciprocal(norm, best))
            link(dve.tensor_tensor(z[:, :, :], z[:, :, :], each_token(norm), ALU.mult))
            link(dve.tensor_reduce(best, over_experts(z), AX_X, ALU.add))
            link(dve.reciprocal(norm, best))
            link(dve.tensor_tensor(prob[:, :, :], z[:, :, :], each_token(norm), ALU.mult))
            for n, (pick, p) in enumerate(((first, p0), (second, p1))):
                link(dve.tensor_reduce(p, over_experts(prob), AX_X, ALU.max))
                link(dve.tensor_tensor(g0[:, :, :], prob[:, :, :], each_token(p), ALU.is_equal))
                link(dve.tensor_tensor(g0[:, :, :], g0[:, :, :], each_expert(experts[:, 1]), ALU.mult))
                link(dve.tensor_reduce(best, over_experts(g0), AX_X, ALU.max))
                link(dve.tensor_tensor(pick[:, :, :], each_token(best), each_expert(experts[:, 1]), ALU.is_equal))
                if n == 0:
                    link(dve.scalar_tensor_tensor(out=prob[:, :, :], in0=first[:, :, :], scalar=-2.0, in1=prob[:, :, :], op0=ALU.mult, op1=ALU.add))
            link(dve.tensor_tensor(norm, p0, p1, ALU.add))
            link(dve.tensor_scalar(norm, norm, 1e-12, None, ALU.max))
            link(dve.reciprocal(norm, norm))
            dve.tensor_tensor(w0, p0, norm, ALU.mult)
            link(dve.tensor_tensor(w1, p1, norm, ALU.mult))
            dve.tensor_tensor(g0[:, :, :], first[:, :, :], each_token(w0), ALU.mult)
            link(dve.tensor_tensor(g1[:, :, :], second[:, :, :], each_token(w1), ALU.mult))
            dve.tensor_tensor(w_mask[:, :, :], first[:, :, :], second[:, :, :], ALU.add)
            link(dve.tensor_tensor(g0[:, :, :], g0[:, :, :], g1[:, :, :], ALU.add))
            link(dve.tensor_scalar(w_mask[:, :, :], w_mask[:, :, :], -1.0, None, ALU.add))
            link(dve.tensor_tensor(w_mask[:, :, :], w_mask[:, :, :], g0[:, :, :], ALU.add))
            dve.wait_ge(rows_copied, NS + 1)
            dve.tensor_copy(rows[:, :, COL_W0], w0)
            dve.tensor_copy(rows[:, :, COL_W1], w1)
            dve.tensor_copy(rows[:, :, COL_TOK], token[:, :])
            dve.tensor_tensor(g0[:, :, :], first[:, :, :], each_expert(experts[:, 0]), ALU.mult)
            dve.memset(bound[:, :], 0).then_inc(search, 1)
            link(dve.memset(bit[:, :], 1 << (BITS - 1)))
            dve.tensor_reduce(rows[:, :, COL_E0], over_experts(g0), AX_X, ALU.add).then_inc(rows_ready, 1)

            with dve.Fori(0, BITS) as r:
                dve.wait_ge(search, 6 * r + 1)
                dve.tensor_tensor(cand[:, :], bound[:, :], bit[:, :], ALU.bitwise_or).then_inc(search, 1)
                dve.wait_ge(search, 6 * r + 2)
                dve.tensor_tensor(g0[:, :, :], w_mask[:, :, :], each_expert(cand[:, :].bitcast(F32)), ALU.is_ge).then_inc(search, 1)
                dve.wait_ge(search, 6 * r + 3)
                with nc.allow_low_precision(reason="counts up to the 32 tiles are exact in bfloat16"):
                    dve.tensor_reduce(count[:, :], g0[:, :, :], AX_X, ALU.add).then_inc(search, 1)
                dve.wait_ge(counted, r + 1)
                dve.tensor_scalar(over[:, :], bank_z[:, 0:E_N], float(CAP), None, ALU.is_ge).then_inc(search, 1)
                dve.wait_ge(search, 6 * r + 5)
                dve.tensor_scalar(bit[:, :], bit[:, :], 1, None, ALU.logical_shift_right).then_inc(search, 1)
                dve.copy_predicated(bound[:, :], over[:, :], cand[:, :]).then_inc(search, 1)
            dve.wait_ge(search, 6 * BITS + 1)
            limit = each_expert(bound[:, :].bitcast(F32))
            dve.tensor_tensor(kept[:, :, :], w_mask[:, :, :], limit, ALU.is_gt)
            link(dve.tensor_tensor(g1[:, :, :], w_mask[:, :, :], limit, ALU.is_equal))

            def before(mark, n):
                dve.tensor_copy(marks[:, :, :], mark[:, :, :]).then_inc(marked, 1)
                dve.wait_ge(summed, n + 1)
                for e in range(E_N):
                    ins = dve.tensor_tensor_scan(prob[:, e], ones[:, 0:NT], bank_z[:, e * NT:(e + 1) * NT], 0.0, ALU.mult, ALU.add)
                link(ins)
                totals = bank_z[:, 0:E_N * NT].rearrange("p (e t) -> p e t", e=E_N)
                inner = bank_r[:, :, :].rearrange("p a b -> p (a b)")[:, 0:E_N * NT].rearrange("p (e t) -> p e t", e=E_N)
                link(dve.tensor_tensor(g0[:, :, :], prob[:, :, :], totals, ALU.subtract))
                link(dve.tensor_tensor(g0[:, :, :], g0[:, :, :], inner, ALU.add))

            before(kept, 0)
            link(dve.tensor_scalar(room[:, :], prob[:, :, NT - 1], -1.0, float(CAP), ALU.mult, ALU.add))
            before(g1, 1)
            link(dve.tensor_tensor(g0[:, :, :], g0[:, :, :], each_expert(room[:, :]), ALU.is_lt))
            link(dve.tensor_tensor(g1[:, :, :], g1[:, :, :], g0[:, :, :], ALU.mult))
            link(dve.tensor_tensor(kept[:, :, :], kept[:, :, :], g1[:, :, :], ALU.add))
            before(kept, 2)
            link(dve.tensor_tensor(g0[:, :, :], g0[:, :, :], each_expert(experts[:, 2]), ALU.add))
            link(dve.scalar_tensor_tensor(out=g0[:, :, :], in0=kept[:, :, :], scalar=-float(FAR), in1=g0[:, :, :], op0=ALU.mult, op1=ALU.add))
            link(dve.tensor_scalar(g0[:, :, :], g0[:, :, :], float(FAR), None, ALU.add))
            for k, pick in enumerate((first, second)):
                link(dve.tensor_tensor(g1[:, :, :], g0[:, :, :], pick[:, :, :], ALU.mult))
                link(dve.tensor_reduce(slot_f[:, :], over_experts(g1), AX_X, ALU.add))
                dve.tensor_copy(slot[:, k], slot_f[:, :]).then_inc(slots_ready, 1)

            def hidden(s):
                for j in range(JC):
                    n = j % 2
                    dve.wait_ge(h_act, s * JC + j + 1)
                    if j >= 2:
                        dve.wait_ge(y_done, s * JC + j - 1)
                    dve.tensor_copy(h_hi[n][:, :], h_f[n][:, :]).then_inc(h_high, 1)
                    dve.wait_ge(h_high, s * JC + j + 1)
                    dve.tensor_tensor(h_lo[n][:, :], h_f[n][:, :], h_hi[n][:, :].bitcast(F32), ALU.subtract).then_inc(h_ready, 1)
                for j in range(SUPER):
                    xb = x_res[:, bass.ds(s * SUPER + j, 1), :].rearrange("p o d -> p (o d)")
                    dve.wait_ge(y_done, (s + 1) * JC)
                    dve.tensor_tensor(xb, acc[j][:, :], xb, ALU.add).then_inc(acc_free, 1)

            for t in range(NT):
                ins = dve.tensor_tensor(x_res[:, t], x_res[:, t], b2_row[:, :], ALU.add)
            link(ins)
            with dve.Fori(0, NS) as s:
                hidden(s)

        @block.tensor
        def _(pe):
            def three(out, terms, start=True, stop=True):
                n, k = len(terms) * 3, 0
                for (lh, ll), (rh, rl) in terms:
                    for lhs, rhs in ((lh, rh), (lh, rl), (ll, rh)):
                        ins = pe.matmul(out, lhs, rhs, start=start and k == 0, stop=stop and k == n - 1)
                        k += 1
                return ins

            pe.wait_ge(small_in, 8 * 16)
            pe.wait_ge(const, 5)

            def turn(s, n):
                pe.wait_ge(xs_ready, s + 1)
                for half in range(2):
                    for c in range(DCH):
                        for j in range(2):
                            ins = pe.transpose(bank_t[half][:, c, j * P:(j + 1) * P], xs[n][:, 2 * half + j, c * P:(c + 1) * P], ident[:, :])
                    ins.then_inc(t_filled, 1)
                pe.wait_ge(xT_ready, 2 * s + 2)
                at = bass.ds(s * SUPER * P, SUPER * P)
                three(bank_z[:, :], [((pw_hi[:, c], pw_lo[:, c]), (xT_hi[:, c, at], xT_lo[:, c, at])) for c in range(DCH)]).then_inc(z_filled, 1)
                pe.wait_ge(z_copied, s + 1)
                for j in range(SUPER):
                    ins = pe.transpose(bank_r[:, j, :], z_turn[:, j * P:(j + 1) * P], ident[:, :])
                ins.then_inc(zr_filled, 1)

            with pe.Fori(0, NS // 2) as k:
                turn(2 * k, 0)
                turn(2 * k + 1, 1)
            pe.wait_ge(rows_ready, 1)
            with pe.Fori(0, BITS) as r:
                pe.wait_ge(search, 6 * r + 4)
                pe.matmul(bank_z[:, 0:E_N], ones[:, :], count[:, :], start=True, stop=True).then_inc(counted, 1)
            for n in range(3):
                pe.wait_ge(marked, n + 1)
                flat = marks[:, :, :].rearrange("p e t -> p (e t)")
                pe.matmul(bank_z[:, 0:E_N * NT], ones[:, :], flat, start=True, stop=True)
                pe.matmul(bank_r[:, :, :].rearrange("p a b -> p (a b)")[:, 0:E_N * NT], tri[:, :], flat, start=True, stop=True).then_inc(summed, 1)

            pe.wait_ge(w_done, len(pieces))

            def shared(s):
                at = bass.ds(s * SUPER * P, SUPER * P)
                for j in range(JC + 1):
                    if j < JC:
                        if j >= 2:
                            pe.wait_ge(h_act, s * JC + j - 1)
                        three(bank_h[j % 2][:, :, :].rearrange("p a b -> p (a b)"),
                              [((w1_hi[:, c, j * P:(j + 1) * P], w1_lo[:, c, j * P:(j + 1) * P]), (xT_hi[:, c, at], xT_lo[:, c, at])) for c in range(DCH)]).then_inc(h_filled, 1)
                    if j >= 1:
                        k = j - 1
                        pe.wait_ge(h_ready, s * JC + k + 1)
                        for tt in range(SUPER):
                            cols = slice(tt * P, (tt + 1) * P)
                            ins = three(acc[tt][:, :], [((h_hi[k % 2][:, cols], h_lo[k % 2][:, cols]), (w2_hi[:, k], w2_lo[:, k]))], start=(k == 0), stop=(k == JC - 1))
                        ins.then_inc(y_done, 1)

            with pe.Fori(0, NS) as s:
                shared(s)


def run_experts(nc, ctx0, dram):
    JC = EH // P
    BATCHES = [(0, 4), (4, 4), (8, 2)]
    CH = len(BATCHES)
    BODY = 2 * CH
    BODIES = E_N // 2
    with ExitStack() as ctx:
        def sb(name, shape, dt=F32):
            return ctx.enter_context(nc.sbuf_tensor(name, shape, dt))

        def psum(name, shape):
            return ctx.enter_context(nc.psum_tensor(name, shape, F32))

        def sem(name):
            return ctx0.enter_context(nc.semaphore(name))

        ident = sb("ident3", [P, P])
        experts = sb("experts3", [P, 3, E_N])
        b1 = [sb(f"fc1_b{n}", [P, JC]) for n in range(2)]
        w_raw = sb("fc_raw", [P, 2, DCH * EH])
        w_hi = [sb(f"fc_hi{n}", [P, 2, DCH * EH], F32R) for n in range(2)]
        w_lo = [sb(f"fc_lo{n}", [P, 2, DCH * EH], F32R) for n in range(2)]
        b2_row = [sb(f"fc2_b{n}", [P, D]) for n in range(2)]
        xe = [sb(f"xe{n}", [P, 4, ROW]) for n in range(2)]
        xeT_hi = [sb(f"xeT_hi{n}", [P, DCH, 4 * P], F32R) for n in range(2)]
        xeT_lo = [sb(f"xeT_lo{n}", [P, DCH, 4 * P], F32R) for n in range(2)]
        mine = sb("mine", [P, 4]); other = sb("other", [P, 4]); part0 = sb("part0", [P, 4]); part1 = sb("part1", [P, 4])
        weight = [sb(f"weight{n}", [P, 4]) for n in range(3)]
        away = sb("away", [P, 4]); tok_f = sb("tok_f", [P, 4])
        tok = [sb(f"tok{n}", [P, 4], U32) for n in range(3)]
        h_f = [sb(f"e_h_f{n}", [P, 4 * P]) for n in range(2)]
        h_hi = [sb(f"e_h_hi{n}", [P, 4 * P], F32R) for n in range(3)]
        h_lo = [sb(f"e_h_lo{n}", [P, 4 * P], F32R) for n in range(3)]
        y = [sb(f"y{n}", [P, 4, D]) for n in range(2)]
        y_w = [sb(f"y_w{n}", [P, 4, D]) for n in range(2)]

        bank_t = [psum(f"e_bank_t{n}", [P, DCH, 2 * P]) for n in range(2)]
        bank_h = [psum(f"e_bank_h{n}", [P, 4 * P]) for n in range(2)]
        acc = [[psum(f"e_acc{n}{i}", [P, 2, D]) for i in range(2)] for n in range(2)]

        small_in = sem("e_small"); w_in = sem("e_w_in"); b2_in = [sem("e_b2_0"), sem("e_b2_1")]
        b1_in = [sem("e_b1_0"), sem("e_b1_1")]
        sp_past = sem("e_sp_past"); pool_past = sem("e_pool_past")
        w_high = sem("e_w_high"); w_ready = sem("e_w_ready")
        xe_in = [sem("e_xe0"), sem("e_xe1")]
        t_filled = sem("e_t_filled"); t_high = sem("e_t_high"); t_ready = sem("e_t_ready")
        picked = sem("e_picked"); slot_info = sem("e_slot_info")
        h_filled = sem("e_h_filled"); h_act = sem("e_h_act"); h_high = sem("e_h_high"); h_ready = sem("e_h_ready")
        y_done = sem("e_y_done"); y_sum = sem("e_y_sum"); y_ready = sem("e_y_ready")
        added = [sem("e_added0"), sem("e_added1")]

        def chunks_before(k, m, p):
            return CH * k + sum(1 for q in range(m) if q % 2 == p)

        def tiles_through(k, m):
            if m < 0:
                k, m = k - 1, m + BODY
            per_body = sum(BATCHES[q % CH][1] for q in range(m % 2, BODY, 2))
            return per_body * k + sum(BATCHES[q % CH][1] for q in range(m % 2, m + 1, 2))

        def bodies(eng, body):
            body(0)
            with eng.Fori(1, BODIES - 1) as k:
                body(k)
            body(BODIES - 1)

        def ring(m, j):
            return (JC * m + j) % 3

        def precedes(k, m):
            if m:
                return k, m - 1
            return None if isinstance(k, int) and k == 0 else (k - 1, BODY - 1)

        def follows(k, m, ahead):
            if m + ahead < BODY:
                return k, m + ahead
            if isinstance(k, int) and k == BODIES - 1:
                return None
            return k + 1, m + ahead - BODY

        block = ctx.enter_context(nc.Block())

        @block.sync
        def _(sp):
            sp.dma_start(ident[:, :], dram["ident"]).then_inc(small_in, 16)
            sp.dma_start(experts[:, :, :], dram["experts"]).then_inc(small_in, 16)

            def load_weights(e, n):
                sp.dma_start(w_raw[:, :, :], dram["fcT"][bass.ds(e, 1)].rearrange("o p a b -> p (o a) b")).then_inc(w_in, 16)
                sp.dma_start(b2_row[n][:, :], dram["fc2_b"][bass.ds(e, 1)].rearrange("o d -> (o d)").partition_broadcast(P)).then_inc(b2_in[n], 16)
                sp.dma_start(b1[n][:, :], dram["fc1_b"][bass.ds(e, 1)].rearrange("o p j -> p (o j)")).then_inc(b1_in[n], 16)

            def load_chunk(k, m):
                e = 2 * k + m // CH
                first, tiles = BATCHES[m % CH]
                src = dram["slots"].rearrange("(e t p) r -> p (e t) r", e=E_N, p=P)[:, bass.ds(e * (CAP // P) + first, tiles)]
                sp.dma_start(xe[m % 2][:, 0:tiles], src).then_inc(xe_in[m % 2], 16)

            load_chunk(0, 0)
            load_weights(0, 0)
            load_chunk(0, 1)

            def body(k):
                for m in range(BODY):
                    n = BODY * k + m
                    if m % CH == 0:
                        e = 2 * k + m // CH
                        if follows(k, m, CH):
                            if isinstance(n, int) and n == 0:
                                sp.wait_ge(w_ready, 1)
                            else:
                                sp.wait_ge(y_sum, n)
                            sp.sem_inc(sp_past, 1)
                            load_weights(e + 1, (m // CH + 1) % 2)
                    nxt = follows(k, m, 2)
                    if nxt:
                        sp.wait_ge(t_filled, n + 1)
                        sp.wait_ge(slot_info, n + 1)
                        sp.sem_inc(sp_past, 1)
                        load_chunk(*nxt)

            bodies(sp, body)

        @block.gpsimd
        def _(pool):
            def low_weights(e, n):
                pool.wait_ge(w_high, e + 1)
                pool.tensor_tensor(w_lo[n][:, :, :], w_raw[:, :, :], w_hi[n][:, :, :].bitcast(F32), ALU.subtract).then_inc(w_ready, 1)

            low_weights(0, 0)

            def body(k):
                for m in range(BODY):
                    n = BODY * k + m
                    if m % CH == 1 and follows(k, m, CH):
                        low_weights(2 * k + m // CH + 1, (m // CH + 1) % 2)
                    pool.wait_ge(y_ready, n + 1)
                    pool.sem_inc(pool_past, 1)
                    for j in range(BATCHES[m % CH][1]):
                        pool.indirect_dma_start(out=dram["out"].rearrange("b s d -> (b s) d"), out_offset=bass.IndirectOffsetOnAxis(ap=tok[m % 3][:, j:j + 1], axis=0),
                                                in_=y_w[m % 2][:, j, :], in_offset=None, bounds_check=N_TOK - 1, oob_is_err=False,
                                                compute_op=ALU.add).then_inc(added[m % 2], 16)
                    if m % CH == CH - 1:
                        pool.wait_ge(added[m % 2], 16 * tiles_through(k, m))
                        pool.wait_ge(added[1 - m % 2], 16 * tiles_through(k, m - 1))

            bodies(pool, body)

        @block.scalar
        def _(act):
            def high(k, m):
                n = BODY * k + m
                tiles = BATCHES[m % CH][1]
                act.wait_ge(t_filled, n + 1)
                if not (isinstance(n, int) and n < 2):
                    act.wait_ge(h_filled, JC * (n - 1))
                for half in range(tiles // 2):
                    ins = act.activation(xeT_hi[m % 2][:, :, half * 2 * P:(half + 1) * 2 * P], bank_t[half][:, :, :], ACT.Identity)
                ins.then_inc(t_high, 1)

            act.wait_ge(small_in, 32)
            high(0, 0)

            def body(k):
                for m in range(BODY):
                    n = BODY * k + m
                    cols = BATCHES[m % CH][1] * P
                    act.wait_ge(b1_in[m // CH], 16 * (k + 1))
                    for j in range(JC):
                        act.wait_ge(h_filled, JC * n + j + 1)
                        if j >= 2 or precedes(k, m):
                            act.wait_ge(h_ready, JC * n + j - 1)
                        act.activation(h_f[j % 2][:, 0:cols], bank_h[j % 2][:, 0:cols], ACT.Gelu,
                                       bias=b1[m // CH][:, j:j + 1]).then_inc(h_act, 1)
                        if j == 1 and follows(k, m, 1):
                            high(*follows(k, m, 1))

            bodies(act, body)

        @block.vector
        def _(dve):
            def high_weights(e, n):
                dve.wait_ge(w_in, 16 * (e + 1))
                dve.tensor_copy(w_hi[n][:, :, :], w_raw[:, :, :]).then_inc(w_high, 1)

            def low(k, m):
                n = BODY * k + m
                tiles = BATCHES[m % CH][1]
                dve.wait_ge(t_high, n + 1)
                for half in range(tiles // 2):
                    at = slice(half * 2 * P, (half + 1) * 2 * P)
                    ins = dve.tensor_tensor(xeT_lo[m % 2][:, :, at], bank_t[half][:, :, :], xeT_hi[m % 2][:, :, at].bitcast(F32), ALU.subtract)
                ins.then_inc(t_ready, 1)

            def slot_values(k, m):
                n = BODY * k + m
                e = 2 * k + m // CH
                t = BATCHES[m % CH][1]
                src = xe[m % 2]
                PICKS = 4
                dve.wait_ge(xe_in[m % 2], 16 * (chunks_before(k, m, m % 2) + 1))
                dve.tensor_scalar(mine[:, 0:t], src[:, 0:t, COL_E0], experts[:, 0, bass.ds(e, 1)], None, ALU.is_equal)
                dve.tensor_scalar(away[:, 0:t], src[:, 0:t, COL_TOK], 0.0, float(FAR), ALU.is_equal, ALU.mult).then_inc(picked, 1)
                dve.wait_ge(picked, PICKS * n + 1)
                dve.tensor_scalar(other[:, 0:t], mine[:, 0:t], -1.0, 1.0, ALU.mult, ALU.add)
                dve.tensor_tensor(part0[:, 0:t], src[:, 0:t, COL_W0], mine[:, 0:t], ALU.mult)
                dve.scalar_tensor_tensor(out=tok_f[:, 0:t], in0=src[:, 0:t, COL_TOK], scalar=-1.0, in1=away[:, 0:t], op0=ALU.add, op1=ALU.add).then_inc(picked, 1)
                dve.wait_ge(picked, PICKS * n + 2)
                dve.tensor_tensor(part1[:, 0:t], src[:, 0:t, COL_W1], other[:, 0:t], ALU.mult).then_inc(picked, 1)
                if not (isinstance(n, int) and n < 3):
                    dve.wait_ge(added[(m - 3) % 2], 16 * tiles_through(k, m - 3))
                dve.tensor_copy(tok[m % 3][:, 0:t], tok_f[:, 0:t]).then_inc(picked, 1)
                dve.wait_ge(picked, PICKS * n + 4)
                dve.tensor_tensor(weight[m % 3][:, 0:t], part0[:, 0:t], part1[:, 0:t], ALU.add).then_inc(slot_info, 1)

            dve.wait_ge(small_in, 32)
            high_weights(0, 0)
            low(0, 0)
            slot_values(0, 0)

            def send(k, m):
                n = BODY * k + m
                tiles = BATCHES[m % CH][1]
                dve.wait_ge(b2_in[m // CH], 16 * (k + 1))
                dve.wait_ge(y_done, JC * (n + 1))
                for i in range(tiles // 2):
                    ins = dve.tensor_tensor(y[m % 2][:, 2 * i:2 * i + 2], acc[m % 2][i][:, :, :], b2_row[m // CH][:, None, :].to_broadcast([P, 2, D]), ALU.add)
                ins.then_inc(y_sum, 1)
                dve.wait_ge(y_sum, n + 1)
                dve.wait_ge(slot_info, n + 1)
                if not (isinstance(n, int) and n < 2):
                    dve.wait_ge(added[m % 2], 16 * tiles_through(k, m - 2))
                for j in range(tiles):
                    ins = dve.tensor_scalar(y_w[m % 2][:, j], y[m % 2][:, j], weight[m % 3][:, j:j + 1], None, ALU.mult)
                ins.then_inc(y_ready, 1)

            def body(k):
                for m in range(BODY):
                    n = BODY * k + m
                    cols = BATCHES[m % CH][1] * P
                    for j in range(JC):
                        b = ring(m, j)
                        dve.wait_ge(h_act, JC * n + j + 1)
                        if j == 3 or precedes(k, m):
                            dve.wait_ge(y_done, JC * n + j - 2)
                        dve.tensor_copy(h_hi[b][:, 0:cols], h_f[j % 2][:, 0:cols]).then_inc(h_high, 1)
                        dve.wait_ge(h_high, JC * n + j + 1)
                        dve.tensor_tensor(h_lo[b][:, 0:cols], h_f[j % 2][:, 0:cols], h_hi[b][:, 0:cols].bitcast(F32), ALU.subtract).then_inc(h_ready, 1)
                        if j == 1:
                            if follows(k, m, 1):
                                low(*follows(k, m, 1))
                            if precedes(k, m):
                                send(*precedes(k, m))
                            if follows(k, m, 1):
                                slot_values(*follows(k, m, 1))
                        if j == 2 and m % CH == 1 and follows(k, m, CH):
                            high_weights(2 * k + m // CH + 1, (m // CH + 1) % 2)

            bodies(dve, body)
            send(BODIES - 1, BODY - 1)

        @block.tensor
        def _(pe):
            def three(out, terms, start=True, stop=True):
                n, k = len(terms) * 3, 0
                for (lh, ll), (rh, rl) in terms:
                    for lhs, rhs in ((lh, rh), (lh, rl), (ll, rh)):
                        ins = pe.matmul(out, lhs, rhs, start=start and k == 0, stop=stop and k == n - 1)
                        k += 1
                return ins

            def turn(k, m):
                tiles = BATCHES[m % CH][1]
                pe.wait_ge(xe_in[m % 2], 16 * (chunks_before(k, m, m % 2) + 1))
                for half in range(tiles // 2):
                    for c in range(DCH):
                        for j in range(2):
                            ins = pe.transpose(bank_t[half][:, c, j * P:(j + 1) * P], xe[m % 2][:, 2 * half + j, c * P:(c + 1) * P], ident[:, :])
                ins.then_inc(t_filled, 1)

            pe.wait_ge(small_in, 32)
            turn(0, 0)

            def up(k, m, j):
                n = BODY * k + m
                f, cols = m // CH, BATCHES[m % CH][1] * P
                if j == 0:
                    pe.wait_ge(t_ready, n + 1)
                    pe.wait_ge(w_ready, 2 * k + f + 1)
                if j >= 2 or precedes(k, m):
                    pe.wait_ge(h_act, JC * n + j - 1)
                w = [slice(c * EH + j * P, c * EH + (j + 1) * P) for c in range(DCH)]
                three(bank_h[j % 2][:, 0:cols], [((w_hi[f][:, 0, w[c]], w_lo[f][:, 0, w[c]]), (xeT_hi[m % 2][:, c, 0:cols], xeT_lo[m % 2][:, c, 0:cols])) for c in range(DCH)]).then_inc(h_filled, 1)

            def down(k, m, j):
                n = BODY * k + m
                f, tiles = m // CH, BATCHES[m % CH][1]
                pe.wait_ge(h_ready, JC * n + j + 1)
                if j == 0 and not (isinstance(n, int) and n < 2):
                    pe.wait_ge(y_sum, n - 1)
                b = ring(m, j)
                wd = slice(j * D, (j + 1) * D)
                for tt in range(tiles):
                    at = slice(tt * P, (tt + 1) * P)
                    for q, (lhs, rhs) in enumerate(((h_hi, w_hi), (h_hi, w_lo), (h_lo, w_hi))):
                        ins = pe.matmul(acc[m % 2][tt // 2][:, tt % 2], lhs[b][:, at], rhs[f][:, 1, wd], start=(j == 0 and q == 0 and tt % 2 == 0),
                                        stop=(j == JC - 1 and q == 2), skip_group_check=True)
                ins.then_inc(y_done, 1)

            def body(k):
                for m in range(BODY):
                    for j in range(JC):
                        up(k, m, j)
                        if j == 1 and follows(k, m, 1):
                            turn(*follows(k, m, 1))
                        if j >= 2:
                            down(k, m, j - 2)
                        elif precedes(k, m):
                            down(*precedes(k, m), JC + j - 2)

            bodies(pe, body)
            down(BODIES - 1, BODY - 1, JC - 2)
            down(BODIES - 1, BODY - 1, JC - 1)


def moe_block(nc, dram):
    with ExitStack() as ctx:
        with nc.sbuf_tensor("x_res", [P, NT, D], F32) as x_res:
            attention(nc, ctx, dram, x_res)
            route_and_shared(nc, ctx, dram, x_res)
        run_experts(nc, ctx, dram)


def kernel(**inputs):
    import concourse.bacc as bacc
    from concourse.bass_utils import run_bass_kernel_spmd

    att = {k[len("L0_xcond_"):]: np.asarray(v) for k, v in inputs.items() if k.startswith("L0_xcond_")}
    ffn = {k[len("L0_ffn_"):]: np.asarray(v) for k, v in inputs.items() if k.startswith("L0_ffn_")}
    sel, one_rows, ident = consts()
    tri, experts, token = route_consts()

    def columns(w, chunks):
        return w.reshape(w.shape[0], chunks, P).transpose(2, 1, 0)

    fc1 = ffn["fc1_w"].reshape(E_N, EH, DCH, P).transpose(0, 3, 2, 1).reshape(E_N, P, DCH * EH)
    fc2 = ffn["fc2_w"].reshape(E_N, D, EH // P, P).transpose(0, 3, 2, 1).reshape(E_N, P, EH // P * D)
    arrays = {
        "x": inputs["x"],
        "ctxT": np.transpose(np.asarray(inputs["ctx_1024"]), (0, 2, 1)),
        "tau": inputs["condB_tau"],
        "delta": inputs["fside_BxS2_0"],
        "WqT": att["Wq"].T, "WkT": att["Wk"].T, "WvT": att["Wv"].T, "WoT": att["Wo"].T,
        "b_qk": np.stack([att["bq"], att["bk"]]).reshape(2, DCH, P).transpose(2, 0, 1),
        "bv": att["bv"], "bo": att["bo"],
        "sel": sel, "one_rows": one_rows, "ident": ident,
        "pw": columns(ffn["proj_w"], DCH),
        "pb_eb": np.broadcast_to(np.stack([ffn["proj_b"], ffn["expert_bias"]])[None], (P, 2, E_N)),
        "sh1T": columns(ffn["sh1_w"], DCH).reshape(P, DCH * SH),
        "sh1_b": ffn["sh1_b"].reshape(SH // P, P).T,
        "sh2T": columns(ffn["sh2_w"], SH // P).reshape(P, SH // P * D),
        "sh2_b": ffn["sh2_b"],
        "fcT": np.stack([fc1, fc2], axis=2),
        "fc1_b": ffn["fc1_b"].reshape(E_N, EH // P, P).transpose(0, 2, 1),
        "fc2_b": ffn["fc2_b"],
        "tri": tri, "experts": experts, "token": token,
    }
    nc = bacc.Bacc("TRN2", target_bir_lowering=False, num_devices=1)
    given, dram = {}, {}
    for name, a in arrays.items():
        a = np.ascontiguousarray(a)
        given[f"in_{name}_dram"] = a
        dram[name] = nc.dram_tensor(f"in_{name}_dram", a.shape, mybir.dt.from_np(a.dtype), kind="ExternalInput").ap()
    dram["delta_hl"] = nc.dram_tensor("delta_hl_dram", (B, 2, S), F32, kind="Internal").ap()
    dram["slots"] = nc.dram_tensor("slots_dram", (E_N * CAP, ROW), F32, kind="Internal").ap()
    dram["out"] = nc.dram_tensor("out_dram", (B, S, D), F32, kind="ExternalOutput").ap()
    moe_block(nc, dram)
    r = run_bass_kernel_spmd(nc, [given], core_ids=[0])
    return r.results[0]["out_dram"]
```

```python
from contextlib import ExitStack

import numpy as np

import concourse.bass as bass
from concourse import mybir

F32 = mybir.dt.float32
F32R = mybir.dt.float32r
BF16 = mybir.dt.bfloat16
U32 = mybir.dt.uint32
ALU = mybir.AluOpType
ACT = mybir.ActivationFunctionType
AX_X = mybir.AxisListType.X

P = 128
B, S, D, H = 16, 256, 256, 16
DK = D // H
EPS = 1e-5
TOK_TILES = S // P
DCH = D // P
NT = B * TOK_TILES
PAIRS = H // 2
HALF = P // 2
QUADS = H // 4
ROW_MAX = 3 * DK
ROW_DELTA = ROW_MAX + 2
STEPS = 11
MAX_STEPS = (0, 1, 2, 3, 4, 5, 6, 7)
TURN_STEPS = (6, 10)


def consts():
    sel = np.zeros((4, P, PAIRS // 2, P), np.float32)
    parts = {0: (0, 2), 1: (1,), 2: (0, 1), 3: (2,)}
    for n, blocks in parts.items():
        for s in range(PAIRS // 2):
            for par in range(2):
                for blk in blocks:
                    for d in range(DK):
                        sel[n, (2 * s + par) * DK + d, s, par * HALF + blk * DK + d] = 1.0
    rows = np.zeros((P, 2), np.float32)
    for par in range(2):
        rows[par * HALF + ROW_DELTA:par * HALF + ROW_DELTA + 2, 0] = 1.0
        rows[par * HALF + ROW_MAX:par * HALF + ROW_MAX + 2, 1] = 1.0
    return sel.transpose(1, 0, 2, 3).copy(), rows, np.eye(P, dtype=np.float32)


def live(b):
    return not isinstance(b, int) or 0 <= b < B


def pipeline(eng, body):
    for i in (-1, 0, 1):
        body(i, i % 2)
    with eng.Fori(1, B // 2 - 1) as n:
        body(2 * n, 0)
        body(2 * n + 1, 1)
    for i in range(B - 2, B + 2):
        body(i, i % 2)


def attention(nc, ctx0, dram, x_res, res_stats, common):
    with ExitStack() as ctx:
        def sb(name, shape, dt=F32):
            return ctx.enter_context(nc.sbuf_tensor(name, shape, dt))

        def psum(name, shape):
            return ctx.enter_context(nc.psum_tensor(name, shape, F32))

        def sem(name):
            return ctx0.enter_context(nc.semaphore(name))

        w_raw = sb("w_raw", [P, 4, DCH, D])
        w_hi = sb("w_hi", [P, 4, DCH, D], F32R)
        w_lo = sb("w_lo", [P, 4, DCH, D], F32R)
        WQ, WK, WV, WO = range(4)
        sel_raw = w_raw[:, :, :, :].rearrange("p a c d -> p (a c d)").rearrange(
            "p (n s m) -> p n s m", n=4, s=PAIRS // 2)
        sel = sb("sel", [P, 4, PAIRS // 2, P], F32R)
        one_rows = sb("one_rows", [P, 2])
        ident = common["ident"]
        b_qk = sb("b_qk", [P, 2, DCH])
        bv_row = sb("bv_row", [P, D])
        bo_row = sb("bo_row", [P, D])
        eps_exp = sb("eps_exp", [P, 2, TOK_TILES])
        delta = sb("delta", [B, S])
        delta_hl = sb("delta_hl", [B, 2, S], F32R)
        stats = sb("stats", [P, TOK_TILES, 6])
        mean_var = sb("mean_var", [P, TOK_TILES, 2])
        rstd = sb("rstd", [P, 2, TOK_TILES])
        xn = sb("xn", [P, TOK_TILES, D])
        xnT_hi = sb("xnT_hi", [P, DCH, S], F32R)
        xnT_lo = sb("xnT_lo", [P, DCH, S], F32R)
        ctx_raw = sb("ctx_raw", [P, 2, DCH, S])
        ctx_hi = sb("ctx_hi", [P, 2, DCH, S], F32R)
        ctx_lo = sb("ctx_lo", [P, 2, DCH, S], F32R)
        tau = sb("tau", [P, 2])
        tau_bq = sb("tau_bq", [P, 2, DCH])
        q_f = sb("q_f", [P, 2, S])
        k_f = sb("k_f", [P, 2, S])
        q_hi = sb("q_hi", [P, 2, S], F32R)
        q_lo = sb("q_lo", [P, 2, S], F32R)
        k_hi = sb("k_hi", [P, 2, S], F32R)
        k_lo = sb("k_lo", [P, 2, S], F32R)
        q_st = [sb(f"q_st{n}", [P, PAIRS, S], F32R) for n in range(2)]
        k_st = [sb(f"k_st{n}", [P, H, S], F32R) for n in range(2)]
        row_max = sb("row_max", [P, TOK_TILES, 2, 2, PAIRS // 2])
        max_hi = [sb(f"max_hi{n}", [H // 2, S], F32R) for n in range(2)]
        max_lo = [sb(f"max_lo{n}", [H // 2, S], F32R) for n in range(2)]
        v1 = [sb(f"v1_{n}", [P, TOK_TILES, H, 32]) for n in range(2)]
        probs = sb("probs", [P, 8, TOK_TILES, S])
        u = sb("u", [P, QUADS, S])
        recip = sb("recip", [P, TOK_TILES, H])
        o = sb("o", [P, TOK_TILES, D])
        oT_hi = sb("oT_hi", [P, DCH, S], F32R)
        oT_lo = sb("oT_lo", [P, DCH, S], F32R)

        bankA = [psum(f"bankA{n}", [P, 2, S]) for n in range(2)]
        bankM = [psum(f"bankM{n}", [P, 2, S]) for n in range(2)]
        bankS = [psum(f"bankS{n}", [P, 2, S]) for n in range(2)]
        bankV = psum("bankV", [P, 2, S])
        bankD = psum("bankD", [P, 512])

        x_in = [sem("x_in0"), sem("x_in1")]
        w_in = sem("w_in"); sel_in = sem("sel_in"); small_in = sem("small_in"); delta_in = sem("delta_in")
        k_clear = [sem("k_clear0"), sem("k_clear1")]; v_clear = sem("v_clear"); eps_set = sem("eps_set")
        w_split = sem("w_split"); sel_ready = sem("sel_ready"); delta_split = sem("delta_split")
        delta_out = sem("delta_out")
        ctx_in = [sem("ctx_in0"), sem("ctx_in1")]
        delta_rows = [[sem(f"delta_rows{n}{half}") for half in range(2)] for n in range(2)]
        ctx_hi_ready = sem("ctx_hi_ready"); ctx_lo_ready = sem("ctx_lo_ready")
        tau_bq_ready = sem("tau_bq_ready")
        stats_ready = sem("stats_ready"); ln_ready = sem("ln_ready"); var_eps = sem("var_eps")
        rstd_ready = sem("rstd_ready"); xn_ready = sem("xn_ready"); bo_added = sem("bo_added")
        a_filled = sem("a_filled")
        xnT_hi_ready = sem("xnT_hi_ready"); xnT_lo_ready = sem("xnT_lo_ready")
        qk_ready = sem("qk_ready"); qk_hi_ready = sem("qk_hi_ready"); qk_lo_ready = sem("qk_lo_ready")
        q_st_ready = sem("q_st_ready"); k_st_ready = sem("k_st_ready")
        m_filled = sem("m_filled"); m_free = [sem("m_free0"), sem("m_free1")]
        maxT_filled = sem("maxT_filled"); max_hi_ready = sem("max_hi_ready")
        max_lo_ready = sem("max_lo_ready"); max_rows = [sem("max_rows0"), sem("max_rows1")]
        v_filled = sem("v_filled"); v_ready = sem("v_ready")
        s_filled = sem("s_filled"); exp_done = sem("exp_done")
        pv_done = sem("pv_done"); u_ready = sem("u_ready")
        d_filled = sem("d_filled"); d_free = sem("d_free"); recip_ready = sem("recip_ready")
        oT_hi_ready = sem("oT_hi_ready"); oT_lo_ready = sem("oT_lo_ready")
        x_res_ready = sem("x_res_ready")

        JOB_XNT, JOB_K, JOB_Q = 0, 1, 2
        JOBS = 3 + 2 * QUADS

        def job_qs(m):
            return 3 + 2 * m

        def job_ks(m):
            return 4 + 2 * m

        def two_loads(b, par):
            return 16 * (b + 2 - par)

        block = ctx.enter_context(nc.Block())

        @block.sync
        def _(sp):
            xv = dram["x"].rearrange("b (c p) d -> p (b c) d", p=P)
            sp.dma_start(x_res[:, 0:4, :], xv[:, 0:4, :]).then_inc(x_in[0], 16)
            sp.dma_start(ident[:, :], dram["ident"]).then_inc(small_in, 16)
            sp.dma_start(one_rows[:, :], dram["one_rows"]).then_inc(small_in, 16)
            sp.dma_start(b_qk[:, :, :], dram["b_qk"]).then_inc(small_in, 16)
            sp.dma_start(bv_row[:, :], dram["bv"].partition_broadcast(P)).then_inc(small_in, 16)
            sp.dma_start(bo_row[:, :], dram["bo"].partition_broadcast(P)).then_inc(small_in, 16)
            sp.dma_start(ctx_raw[:, 0], dram["ctxT"][0].rearrange("(c p) s -> p c s", p=P)).then_inc(ctx_in[0], 16)
            sp.dma_start(tau[:, 0:1], dram["tau"][0:1].partition_broadcast(P)).then_inc(ctx_in[0], 16)
            for n, w in enumerate(("WqT", "WkT", "WvT", "WoT")):
                sp.dma_start(w_raw[:, n], dram[w].rearrange("(c p) d -> p c d", p=P)).then_inc(w_in, 16)
            sp.dma_start(delta[:, :], dram["delta"]).then_inc(delta_in, 16)
            sp.wait_ge(w_split, 2)
            sp.dma_start(sel_raw, dram["sel"]).then_inc(sel_in, 16)
            sp.dma_start(x_res[:, 4:NT, :], xv[:, 4:NT, :]).then_inc(x_in[1], 16)
            sp.wait_ge(delta_split, 2)
            sp.dma_start(dram["delta_hl"], delta_hl[:, :, :].bitcast(F32)).then_inc(delta_out, 16)
            sp.wait_ge(delta_out, 16)

            def load_delta_rows(b, par, half):
                heads = slice(half * H // 2, (half + 1) * H // 2)
                for p in range(2):
                    at = p * HALF + ROW_DELTA
                    dst = k_st[par][at:at + 2, heads, :].rearrange("r (s p) k -> r p s k", p=2)[:, p]
                    src = dram["delta_hl"][bass.ds(b, 1)].rearrange("o r k -> (o r) k")
                    src = src[:, None, :].to_broadcast([2, PAIRS // 2, S])
                    sp.dma_start(dst.bitcast(F32), src).then_inc(delta_rows[par][half], 16)

            def iteration(i, par):
                a, nxt = i + 1, i + 2
                if live(nxt):
                    if live(nxt - 2):
                        sp.wait_ge(qk_lo_ready, 2 * (nxt - 1))
                    sp.dma_start(ctx_raw[:, par], dram["ctxT"][bass.ds(nxt, 1)].rearrange(
                        "o (c p) s -> p (o c) s", p=P)).then_inc(ctx_in[par], 16)
                    sp.dma_start(tau[:, par:par + 1], dram["tau"][bass.ds(nxt, 1)].partition_broadcast(P)).then_inc(ctx_in[par], 16)
                for half in range(2):
                    if live(a):
                        if live(a - 2):
                            sp.wait_ge(s_filled, H * (a - 2) + (half + 1) * H // 2)
                        else:
                            sp.wait_ge(k_clear[1 - par], 1)
                        load_delta_rows(a, 1 - par, half)
                    if live(i):
                        sp.wait_ge(max_hi_ready, 2 * i + half + 1)
                        sp.wait_ge(max_lo_ready, 2 * i + half + 1)
                        for p in range(2):
                            for n, part in enumerate((max_hi[half], max_lo[half])):
                                at = p * HALF + ROW_MAX + n
                                sp.dma_start(q_st[par][at:at + 1, half * PAIRS // 2:(half + 1) * PAIRS // 2, :].bitcast(F32),
                                             part[p * PAIRS // 2:(p + 1) * PAIRS // 2, :].bitcast(F32)).then_inc(max_rows[half], 16)

            pipeline(sp, iteration)

        @block.gpsimd
        def _(pool):
            pool.memset(eps_exp[:, 0], EPS)
            pool.memset(eps_exp[:, 1], -0.5).then_inc(eps_set, 1)
            pool.memset(k_st[0][:, :, :].bitcast(F32), 0.0).then_inc(k_clear[0], 1)
            pool.wait_ge(eps_set, 1)

            def reciprocal_std(b):
                pool.wait_ge(ln_ready, b + 1)
                pool.tensor_tensor(rstd[:, 0], mean_var[:, :, 1], eps_exp[:, 0], ALU.add).then_inc(var_eps, 1)
                pool.wait_ge(var_eps, b + 1)
                pool.tensor_tensor(rstd[:, 1], rstd[:, 0], eps_exp[:, 1], ALU.pow).then_inc(rstd_ready, 1)

            def low_context(b, par):
                pool.wait_ge(ctx_hi_ready, b + 1)
                pool.tensor_tensor(ctx_lo[:, par], ctx_raw[:, par], ctx_hi[:, par].bitcast(F32), ALU.subtract).then_inc(ctx_lo_ready, 1)

            def add_bo(b):
                pool.wait_ge(small_in, 5 * 16)
                pool.wait_ge(xn_ready, b + 1)
                xb = x_res[:, bass.ds(b * TOK_TILES, TOK_TILES), :]
                pool.tensor_tensor(xb, xb, bo_row[:, None, :].to_broadcast([P, TOK_TILES, D]), ALU.add).then_inc(bo_added, 1)

            def iteration(i, par):
                a = i + 1
                if isinstance(i, int) and i == -1:
                    reciprocal_std(0)
                    pool.wait_ge(w_split, 1)
                    pool.tensor_tensor(w_lo[:, :, :, :], w_raw[:, :, :, :], w_hi[:, :, :, :].bitcast(F32), ALU.subtract).then_inc(w_split, 1)
                    low_context(0, 0)
                    iteration_a(a, par)
                    pool.wait_ge(delta_split, 1)
                    pool.tensor_tensor(delta_hl[:, 1], delta[:, :], delta_hl[:, 0].bitcast(F32), ALU.subtract).then_inc(delta_split, 1)
                    pool.memset(k_st[1][:, :, :].bitcast(F32), 0.0).then_inc(k_clear[1], 1)
                    add_bo(0)
                    reciprocal_std(1)
                    for n in range(2):
                        pool.memset(v1[n][:, :, :, :], 0.0).then_inc(v_clear, 1)
                    pool.wait_ge(v_clear, 2)
                    for n in range(2):
                        pool.memset(v1[n][:, :, :, DK:DK + 1], 1.0).then_inc(v_clear, 1)
                    add_bo(1)
                    low_context(1, 1)
                    return
                if live(a):
                    iteration_a(a, par)
                if live(i + 2):
                    reciprocal_std(i + 2)
                    add_bo(i + 2)
                    low_context(i + 2, par)

            def iteration_a(a, par):
                pool.wait_ge(ctx_in[1 - par], two_loads(a, 1 - par))
                pool.wait_ge(small_in, 5 * 16)
                if live(a - 2):
                    pool.wait_ge(qk_ready, 2 * (a - 1))
                pool.tensor_tensor(tau_bq[:, 1 - par], b_qk[:, 0, :], tau[:, 1 - par:2 - par].to_broadcast([P, DCH]), ALU.mult).then_inc(tau_bq_ready, 1)
                for n, (f, hi, lo) in enumerate(((k_f, k_hi, k_lo), (q_f, q_hi, q_lo))):
                    pool.wait_ge(qk_hi_ready, 2 * a + n + 1)
                    pool.tensor_tensor(lo[:, :, :], f[:, :, :], hi[:, :, :].bitcast(F32), ALU.subtract).then_inc(qk_lo_ready, 1)

            pipeline(pool, iteration)

        @block.scalar
        def _(act):
            def iteration(i, par):
                a, sm, d = i + 1, i - 1, i - 2
                for t in range(STEPS):
                    if live(sm) and 2 <= t < 2 + PAIRS:
                        for h in (2 * (t - 2), 2 * (t - 2) + 1):
                            act.wait_ge(s_filled, H * sm + h + 1)
                            if h >= 8:
                                act.wait_ge(pv_done, QUADS * sm + (h - 8) // 4 + 1)
                            elif live(sm - 1):
                                act.wait_ge(pv_done, QUADS * (sm - 1) + (h + 8) // 4 + 1)
                            act.activation(probs[:, h % 8], bankS[h % 2][:, :, :], ACT.Exp, scale=float(DK) ** -0.5).then_inc(exp_done, 1)
                    if live(a):
                        if t == 0:
                            act.wait_ge(a_filled, JOBS * a + JOB_XNT + 1)
                            if live(a - 1):
                                act.wait_ge(a_filled, JOBS * (a - 1) + JOB_Q + 1)
                            act.activation(xnT_hi[:, :, :], bankA[0][:, :, :], ACT.Identity).then_inc(xnT_hi_ready, 1)
                        if t == 1:
                            act.wait_ge(a_filled, JOBS * a + JOB_K + 1)
                            if live(a - 1):
                                act.wait_ge(qk_lo_ready, 2 * (a - 1) + 1)
                            for g in range(2):
                                ins = act.activation(k_f[:, g], bankA[JOB_K % 2][:, g], ACT.Identity, bias=b_qk[:, 1, g:g + 1])
                            ins.then_inc(qk_ready, 1)
                        if t == 1:
                            act.wait_ge(a_filled, JOBS * a + JOB_Q + 1)
                            act.wait_ge(tau_bq_ready, a + 1)
                            if live(a - 1):
                                act.wait_ge(qk_lo_ready, 2 * (a - 1) + 2)
                            for g in range(2):
                                ins = act.activation(q_f[:, g], bankA[JOB_Q % 2][:, g], ACT.Identity, bias=tau_bq[:, 1 - par, g:g + 1], scale=tau[:, 1 - par:2 - par])
                            ins.then_inc(qk_ready, 1)
                        if t >= 4 and t % 2 == 0:
                            m = (t - 4) // 2
                            act.wait_ge(a_filled, JOBS * a + job_qs(m) + 1)
                            if live(a - 2):
                                act.wait_ge(s_filled, H * (a - 2) + 4 * (m + 1))
                            act.activation(q_st[1 - par][:, 2 * m:2 * m + 2], bankA[job_qs(m) % 2][:, :, :], ACT.Identity, bias=one_rows[:, 0:1]).then_inc(q_st_ready, 1)
                            act.wait_ge(a_filled, JOBS * a + job_ks(m) + 1)
                            if not live(a - 2):
                                act.wait_ge(k_clear[1 - par], 1)
                            for p in range(2):
                                rows = slice(p * HALF, p * HALF + ROW_DELTA)
                                ins = act.activation(k_st[1 - par][rows, 4 * m:4 * m + 4].rearrange("r (s p) k -> r p s k", p=2)[:, p],
                                                     bankA[job_ks(m) % 2][rows], ACT.Identity, bias=one_rows[rows, 1:2])
                            ins.then_inc(k_st_ready, 1)
                    if live(d) and t == 5:
                        act.wait_ge(d_filled, 4 * d + 3)
                        if live(d - 1):
                            act.wait_ge(d_filled, 4 * (d - 1) + 4)
                        act.activation(oT_hi[:, :, :].rearrange("p c s -> p (c s)"), bankD[:, :], ACT.Identity).then_inc(oT_hi_ready, 1)
                    if live(i) and t in TURN_STEPS:
                        half = TURN_STEPS.index(t)
                        act.wait_ge(maxT_filled, 2 * i + half + 1)
                        if live(i - 1):
                            act.wait_ge(max_rows[half], 64 * i)
                        act.activation(max_hi[half][:, :], bankD[0:H // 2, 0:S], ACT.Identity, scale=-1.0).then_inc(max_hi_ready, 1)
                    if live(sm) and t in (6, 10):
                        half = (t - 6) // 4
                        act.wait_ge(pv_done, QUADS * sm + 2 * half + 2)
                        if live(sm - 1):
                            act.wait_ge(d_filled, 4 * (sm - 1) + 2)
                        act.activation(u[:, 2 * half:2 * half + 2], bankV[:, :, :], ACT.Identity).then_inc(u_ready, 1)

            act.wait_ge(small_in, 5 * 16)
            pipeline(act, iteration)

        @block.vector
        def _(dve):
            dve.wait_ge(w_in, 64)
            dve.tensor_copy(w_hi[:, :, :, :], w_raw[:, :, :, :]).then_inc(w_split, 1)
            dve.wait_ge(delta_in, 16)
            dve.tensor_copy(delta_hl[:, 0], delta[:, :]).then_inc(delta_split, 1)

            def statistics(b):
                for c in range(TOK_TILES):
                    ins = dve.bn_stats(stats[:, c], x_res[:, bass.ds(b * TOK_TILES + c, 1), :].rearrange("p o d -> p (o d)"))
                ins.then_inc(stats_ready, 1)

            def high_context(b, par):
                dve.wait_ge(ctx_in[par], two_loads(b, par))
                if live(b - 2):
                    dve.wait_ge(v_filled, b - 1)
                dve.tensor_copy(ctx_hi[:, par], ctx_raw[:, par]).then_inc(ctx_hi_ready, 1)

            def mean_variance(b):
                for c in range(TOK_TILES):
                    ins = dve.bn_aggr(mean_var[:, c], stats[:, c])
                ins.then_inc(ln_ready, 1)

            def normalise(b):
                dve.wait_ge(rstd_ready, b + 1)
                if live(b - 1):
                    dve.wait_ge(a_filled, JOBS * (b - 1) + JOB_XNT + 1)
                for c in range(TOK_TILES):
                    ins = dve.tensor_scalar(xn[:, c], x_res[:, bass.ds(b * TOK_TILES + c, 1), :].rearrange("p o d -> p (o d)"),
                                            mean_var[:, c, 0:1], rstd[:, 1, c:c + 1], ALU.subtract, ALU.mult)
                ins.then_inc(xn_ready, 1)

            def iteration(i, par):
                a, d = i + 1, i - 2
                if isinstance(i, int) and i == -1:
                    dve.wait_ge(x_in[0], 16)
                    statistics(0)
                    dve.wait_ge(stats_ready, 1)
                    mean_variance(0)
                    high_context(0, 0)
                    normalise(0)
                for t in range(STEPS):
                    if live(a):
                        if t == 0:
                            dve.wait_ge(xnT_hi_ready, a + 1)
                            dve.tensor_tensor(xnT_lo[:, :, :], bankA[0][:, :, :], xnT_hi[:, :, :].bitcast(F32), ALU.subtract).then_inc(xnT_lo_ready, 1)
                        if t in (2, 3):
                            n = t - 2
                            f, hi = ((k_f, k_hi), (q_f, q_hi))[n]
                            dve.wait_ge(qk_ready, 2 * a + n + 1)
                            if live(a - 1):
                                dve.wait_ge(a_filled, JOBS * a)
                            dve.tensor_copy(hi[:, :, :], f[:, :, :]).then_inc(qk_hi_ready, 1)
                        if t == 3 and isinstance(i, int) and i == -1:
                            dve.wait_ge(sel_in, 16)
                            dve.tensor_copy(sel[:, :, :, :], sel_raw).then_inc(sel_ready, 1)
                    if live(i) and t in MAX_STEPS:
                        pair = MAX_STEPS.index(t)
                        if t == 0 and live(i - 1):
                            dve.wait_ge(maxT_filled, 2 * i)
                        if t == 6 and live(i + 2):
                            dve.wait_ge(stats_ready, i + 3)
                        for c in range(TOK_TILES):
                            dve.wait_ge(m_filled, 2 * PAIRS * i + 2 * pair + c + 1)
                            dve.tensor_reduce(row_max[:, c, pair // (PAIRS // 2), :, pair % (PAIRS // 2)], bankM[c][:, :, :], AX_X, ALU.max).then_inc(m_free[c], 1)
                    if live(i + 2):
                        if t == 5:
                            if isinstance(i, int) and i == 0:
                                dve.wait_ge(x_in[1], 16)
                            statistics(i + 2)
                        if t == 6:
                            if isinstance(i, int) and i == -1:
                                dve.wait_ge(stats_ready, i + 3)
                            mean_variance(i + 2)
                        if t == 7:
                            normalise(i + 2)
                    if live(d) and t in (1, 3):
                        c = t // 2
                        dve.wait_ge(d_filled, 4 * d + c + 1)
                        turned = bankD[:, :].rearrange("p (h k) -> p h k", h=H)
                        dve.reciprocal(recip[:, c], turned[:, :, DK]).then_inc(recip_ready, 1)
                        dve.wait_ge(recip_ready, 2 * d + c + 1)
                        dve.tensor_tensor(o[:, c].rearrange("p (h k) -> p h k", h=H), turned[:, :, 0:DK],
                                          recip[:, c, :, None].to_broadcast([P, H, DK]), ALU.mult).then_inc(d_free, 1)
                    if live(d) and t == 5:
                        dve.wait_ge(oT_hi_ready, d + 1)
                        dve.tensor_tensor(oT_lo[:, :, :].rearrange("p c s -> p (c s)"), bankD[:, :],
                                          oT_hi[:, :, :].rearrange("p c s -> p (c s)").bitcast(F32), ALU.subtract).then_inc(d_free, 1)
                    if live(d) and t == 7:
                        dve.wait_ge(d_filled, 4 * d + 4)
                        dve.wait_ge(bo_added, d + 1)
                        xb = x_res[:, bass.ds(d * TOK_TILES, TOK_TILES), :].rearrange("p c d -> p (c d)")
                        dve.tensor_tensor(xb, bankD[:, :], xb, ALU.add).then_inc(d_free, 1)
                    if live(d) and t == 10:
                        dve.wait_ge(d_free, 4 * d + 4)
                        for c in range(TOK_TILES):
                            tile = bass.ds(d * TOK_TILES + c, 1)
                            dve.bn_stats(res_stats[:, tile, :].rearrange("p o s -> p (o s)"), x_res[:, tile, :].rearrange("p o d -> p (o d)"))
                    if live(i) and t in TURN_STEPS:
                        half = TURN_STEPS.index(t)
                        dve.wait_ge(max_hi_ready, 2 * i + half + 1)
                        if live(i - 1):
                            dve.wait_ge(max_rows[half], 64 * i)
                        dve.scalar_tensor_tensor(out=max_lo[half][:, :], in0=bankD[0:H // 2, 0:S], scalar=-1.0,
                                                 in1=max_hi[half][:, :].bitcast(F32), op0=ALU.mult, op1=ALU.subtract).then_inc(max_lo_ready, 1)
                    if live(i) and t == 9:
                        dve.wait_ge(v_filled, i + 1)
                        if live(i - 2):
                            dve.wait_ge(pv_done, QUADS * (i - 1))
                        else:
                            dve.wait_ge(v_clear, 4)
                        dve.tensor_tensor(v1[par][:, :, :, 0:DK], bankM[1][:, :, :].rearrange("p c (h k) -> p c h k", h=H),
                                          bv_row[:, None, :].to_broadcast([P, TOK_TILES, D]).rearrange("p c (h k) -> p c h k", h=H), ALU.add).then_inc(v_ready, 1)
                    if live(i + 2) and t == 9:
                        high_context(i + 2, par)

            dve.wait_ge(small_in, 5 * 16)
            pipeline(dve, iteration)

        @block.tensor
        def _(pe):
            def three(out, terms):
                n = len(terms) * 3
                k = 0
                for (lh, ll), (rh, rl) in terms:
                    for lhs, rhs in ((lh, rh), (lh, rl), (ll, rh)):
                        ins = pe.matmul(out, lhs, rhs, start=(k == 0), stop=(k == n - 1))
                        k += 1
                return ins

            def project(bank, w, hi, lo):
                for g in range(DCH):
                    cols = slice(g * P, (g + 1) * P)
                    ins = three(bank[:, g], [((w_hi[:, w, c, cols], w_lo[:, w, c, cols]), (hi[:, c], lo[:, c])) for c in range(DCH)])
                return ins

            def stack(bank, m, which, hi, lo):
                for s in range(2):
                    pair = 2 * m + s
                    g, local = pair // (PAIRS // 2), pair % (PAIRS // 2)
                    pe.matmul(bank[:, s], sel[:, 2 * which, local], hi[:, g], start=True, stop=False)
                    ins = pe.matmul(bank[:, s], sel[:, 2 * which + 1, local], lo[:, g], start=False, stop=True)
                return ins

            def turn_maxima(i, half):
                for c in range(TOK_TILES):
                    pe.wait_ge(m_free[c], PAIRS * i + (half + 1) * PAIRS // 2)
                if live(i - 2):
                    pe.wait_ge(d_free, 4 * (i - 2) + 3 + half)
                if half == 1:
                    pe.wait_ge(max_lo_ready, 2 * i + 1)
                elif live(i - 1):
                    pe.wait_ge(max_lo_ready, 2 * i)
                for c in range(TOK_TILES):
                    ins = pe.transpose(bankD[0:H // 2, c * P:(c + 1) * P], row_max[:, c, half].rearrange("p a b -> p (a b)"), ident[:, :])
                ins.then_inc(maxT_filled, 1)

            def iteration(i, par):
                a, sm, d = i + 1, i - 1, i - 2
                for t in range(STEPS):
                    if live(sm) and 2 <= t < 2 + PAIRS:
                        if t in (2, 6):
                            pe.wait_ge(max_rows[t // 6], 64 * (sm + 1))
                        for h in (2 * (t - 2), 2 * (t - 2) + 1):
                            if h >= 2:
                                pe.wait_ge(exp_done, H * sm + h - 1)
                            elif live(sm - 1):
                                pe.wait_ge(exp_done, H * sm + h - 1)
                            for c in range(TOK_TILES):
                                ins = pe.matmul(bankS[h % 2][:, c], k_st[1 - par][:, h, c * P:(c + 1) * P], q_st[1 - par][:, h // 2], start=True, stop=True)
                            ins.then_inc(s_filled, 1)
                    if live(a):
                        if t == 0:
                            pe.wait_ge(xn_ready, a + 1)
                            if live(a - 1):
                                pe.wait_ge(k_st_ready, QUADS * a)
                            for c in range(DCH):
                                for tt in range(TOK_TILES):
                                    ins = pe.transpose(bankA[0][:, c, tt * P:(tt + 1) * P], xn[:, tt, c * P:(c + 1) * P], ident[:, :])
                            ins.then_inc(a_filled, 1)
                        if t == 1:
                            pe.wait_ge(w_split, 2)
                            pe.wait_ge(ctx_hi_ready, a + 1)
                            pe.wait_ge(ctx_lo_ready, a + 1)
                            if live(a - 1):
                                pe.wait_ge(q_st_ready, QUADS * a)
                            project(bankA[JOB_K % 2], WK, ctx_hi[:, 1 - par], ctx_lo[:, 1 - par]).then_inc(a_filled, 1)
                            pe.wait_ge(xnT_lo_ready, a + 1)
                            project(bankA[JOB_Q % 2], WQ, xnT_hi, xnT_lo).then_inc(a_filled, 1)
                    if live(i) and t in MAX_STEPS:
                        pair = MAX_STEPS.index(t)
                        if pair % 2 == 0:
                            m = pair // 2
                            pe.wait_ge(q_st_ready, QUADS * i + m + 1)
                            pe.wait_ge(k_st_ready, QUADS * i + m + 1)
                        if pair % 4 == 0:
                            pe.wait_ge(delta_rows[par][pair // 4], two_loads(i, par))
                        for c in range(TOK_TILES):
                            if pair > 0:
                                pe.wait_ge(m_free[c], PAIRS * i + pair)
                            elif live(i - 1):
                                pe.wait_ge((m_free[0], v_ready)[c], (PAIRS * i, i)[c])
                            for p in range(2):
                                ins = pe.matmul(bankM[c][:, p], q_st[par][:, pair, c * P:(c + 1) * P], k_st[par][:, 2 * pair + p], start=True, stop=True)
                            ins.then_inc(m_filled, 1)
                    if live(a) and t >= 4 and t % 2 == 0:
                        m = (t - 4) // 2
                        if m == 0:
                            pe.wait_ge(qk_lo_ready, 2 * a + 2)
                            pe.wait_ge(qk_ready, 2 * a + 2)
                            pe.wait_ge(sel_ready, 1)
                        else:
                            pe.wait_ge(q_st_ready, QUADS * a + m)
                        stack(bankA[1], m, 0, q_hi, q_lo).then_inc(a_filled, 1)
                        if m:
                            pe.wait_ge(k_st_ready, QUADS * a + m)
                        stack(bankA[0], m, 1, k_hi, k_lo).then_inc(a_filled, 1)
                    if live(d) and t in (1, 3):
                        c = t // 2
                        if c == 0:
                            pe.wait_ge(u_ready, 2 * (d + 1))
                        if c == 1:
                            pe.wait_ge(d_free, 4 * d + 1)
                        elif live(i - 1):
                            pe.wait_ge(max_lo_ready, 2 * i)
                        else:
                            pe.wait_ge(d_free, 4 * d)
                        for g in range(QUADS):
                            ins = pe.transpose(bankD[:, g * P:(g + 1) * P], u[:, g, c * P:(c + 1) * P], ident[:, :])
                        ins.then_inc(d_filled, 1)
                    if live(d) and t == 5:
                        pe.wait_ge(d_free, 4 * d + 2)
                        for g in range(DCH):
                            for c in range(TOK_TILES):
                                ins = pe.transpose(bankD[:, g * S + c * P:g * S + (c + 1) * P], o[:, c, g * P:(g + 1) * P], ident[:, :])
                        ins.then_inc(d_filled, 1)
                    if live(i) and t == TURN_STEPS[0]:
                        turn_maxima(i, 0)
                    if live(d) and t == 7:
                        pe.wait_ge(d_free, 4 * d + 3)
                        if live(i):
                            pe.wait_ge(max_lo_ready, 2 * i + 1)
                        for c in range(TOK_TILES):
                            cols = slice(c * P, (c + 1) * P)
                            ins = three(bankD[:, c * D:(c + 1) * D], [((oT_hi[:, g, cols], oT_lo[:, g, cols]), (w_hi[:, WO, g], w_lo[:, WO, g])) for g in range(DCH)])
                        ins.then_inc(d_filled, 1)
                    if live(sm) and t >= 4 and t % 2 == 0:
                        g = (t - 4) // 2
                        pe.wait_ge(exp_done, H * sm + 4 * (g + 1))
                        if g == 0:
                            pe.wait_ge(v_ready, sm + 1)
                        if g == 2:
                            pe.wait_ge(u_ready, 2 * sm + 1)
                        elif g == 0 and live(sm - 1):
                            pe.wait_ge(u_ready, 2 * sm)
                        for c in range(TOK_TILES):
                            for j in range(4):
                                h = 4 * g + j
                                ins = pe.matmul(bankV[32 * j:32 * j + 32, g % 2], v1[1 - par][:, c, h], probs[:, h % 8, c], start=(c == 0), stop=(c == TOK_TILES - 1),
                                                skip_group_check=True)
                        ins.then_inc(pv_done, 1)
                    if live(i) and t == TURN_STEPS[1]:
                        turn_maxima(i, 1)
                    if live(i) and t == 9:
                        pe.wait_ge(m_free[1], PAIRS * (i + 1))
                        for c in range(TOK_TILES):
                            cols = slice(c * P, (c + 1) * P)
                            ins = three(bankM[1][:, c], [((ctx_hi[:, par, g, cols], ctx_lo[:, par, g, cols]), (w_hi[:, WV, g], w_lo[:, WV, g])) for g in range(DCH)])
                        ins.then_inc(v_filled, 1)

            pe.wait_ge(small_in, 5 * 16)
            pipeline(pe, iteration)


E_N, EH, SH = 8, 512, 1024
CAP = 1280
N_TOK = B * S
SUPER = 4
NS = NT // SUPER
ROW = D + 4
COL_W0, COL_W1, COL_TOK, COL_E0 = D, D + 1, D + 2, D + 3
BITS = 30
BITS_STEP = 2
CANDS = (1 << BITS_STEP) - 1
STEP_INCS = 4 + CANDS
SEARCH_STEPS = 16
FAR = 1 << 14
HALF_SEARCH = [10 + 3 * r for r in range(SEARCH_STEPS)]
HALF_SUMS = (58, 62, 66)
SLOT_TURN = 36


def route_consts():
    p = np.arange(P)
    tri = (p[:, None] < p[None, :]).astype(np.float32)
    experts = np.zeros((P, 3, E_N), np.float32)
    experts[:, 0] = np.arange(E_N)
    experts[:, 1] = E_N - np.arange(E_N)
    experts[:, 2] = CAP * np.arange(E_N)
    token = (np.arange(NT)[None, :] * P + p[:, None] + 1).astype(np.float32)
    return tri, experts, token


def super_live(s):
    return not isinstance(s, int) or 0 <= s < NS


def super_tiles(eng, body):
    body(0, 0)
    body(1, 1)
    with eng.Fori(1, NS // 2 - 1) as k:
        body(2 * k, 0)
        body(2 * k + 1, 1)
    for s in range(NS - 2, NS + 2):
        body(s, s % 2)


def route_and_shared(nc, ctx0, dram, x_res, stats, common):
    with ExitStack() as ctx:
        def sb(name, shape, dt=F32):
            return ctx.enter_context(nc.sbuf_tensor(name, shape, dt))

        def psum(name, shape, dt=F32):
            return ctx.enter_context(nc.psum_tensor(name, shape, dt))

        def sem(name):
            return ctx0.enter_context(nc.semaphore(name))

        rows = sb("rows", [P, NT, ROW])
        xT_hi = sb("xT_hi", [P, DCH, N_TOK], F32R)
        xT_lo = sb("xT_lo", [P, DCH, N_TOK], F32R)
        JC = SH // P
        w1_hi = sb("sh1_hi", [P, DCH, SH], F32R)
        w1_lo = sb("sh1_lo", [P, DCH, SH], F32R)
        w2_hi = sb("sh2_hi", [P, JC, D], F32R)
        w2_lo = sb("sh2_lo", [P, JC, D], F32R)
        b1 = sb("sh1_b", [P, JC])
        b2_row = sb("sh2_b", [P, D])
        pw_raw = sb("pw_raw", [P, DCH, E_N])
        pw_hi = sb("pw_hi", [P, DCH, P], F32R)
        pw_lo = sb("pw_lo", [P, DCH, P], F32R)
        pb_eb = sb("pb_eb", [P, 2, E_N])
        ident, experts, scratch, out_sem = (common[n] for n in ("ident", "experts", "scratch", "x_out"))
        tri_f = sb("tri_f", [P, P])
        tri = sb("tri", [P, P], BF16)
        ones = sb("ones", [P, P], BF16)
        token = sb("token", [P, NT])
        eps_exp = sb("eps_exp2", [P, 2, NT])
        xs = [sb(f"xs{n}", [P, SUPER, D]) for n in range(2)]
        h_f = xs[0][:, :, :].rearrange("p (n a) d -> p n (a d)", n=2)
        HB = 4
        h_parts = sb("h_parts", [P, HB, 2, SUPER * P], F32R)
        zero_row = sb("zero_row", [P, ROW])

        bank_t = [psum(f"bank_t{n}", [P, DCH, 2 * P]) for n in range(2)]
        bank_z = psum("bank_z", [P, SUPER * P])
        bank_r = psum("bank_r", [P, SUPER, P])
        acc = [[psum(f"acc{n}{m}", [P, 2, D]) for m in range(SUPER // 2)] for n in range(2)]
        bank_h = bank_t

        mu = sb("mu", [P, NT]); var = sb("var", [P, NT]); dif = sb("dif", [P, NT])
        rstd = sb("rstd2", [P, NT])

        grids = scratch[:, 0:(8 + CANDS) * E_N * NT].rearrange("p (n e t) -> p n e t", n=8 + CANDS, e=E_N)
        prob, g0, g1, first, second, w_mask, kept = (grids[:, n] for n in range(7))
        reached, z = grids[:, 7:7 + CANDS], grids[:, 7 + CANDS]
        z_turn = scratch[:, (8 + CANDS) * E_N * NT:(8 + CANDS) * E_N * NT + SUPER * P]
        marks = sb("marks", [P, E_N, NT], BF16)
        per_tok = sb("per_tok", [P, 6, NT])
        slot_f = sb("slot_f", [P, NT])
        slot = sb("slot", [P, 2, NT], U32)
        bound = sb("bound", [P, E_N], U32)
        cand = sb("cand", [P, CANDS, E_N], U32)
        step = sb("step", [P, CANDS, E_N], U32)
        over = sb("over", [P, CANDS, E_N], U32)
        count = sb("count", [P, CANDS * E_N], BF16)
        room = sb("room", [P, E_N])

        small_in = sem("f_small"); w_staged = [sem("f_w_staged0"), sem("f_w_staged1")]; w_high = sem("f_w_high"); w_done = sem("f_w_done")
        const = sem("f_const"); chain = sem("f_chain"); pool_ln = sem("f_pool_ln"); rstd_ready = sem("f_rstd")
        xs_ready = sem("f_xs"); rows_copied = sem("f_rows_copied"); t_filled = sem("f_t_filled")
        xT_hi_ready = sem("f_xT_hi"); xT_ready = sem("f_xT"); z_filled = sem("f_z_filled"); z_copied = sem("f_z_copied")
        zr_filled = sem("f_zr_filled"); z_ready = sem("f_z_ready")
        sig_in = sem("f_sig_in"); sig_done = sem("f_sig")
        search = sem("f_search"); counted = sem("f_counted")
        marked = sem("f_marked"); summed = sem("f_summed"); pw_split = sem("f_pw_split"); slots_ready = sem("f_slots"); rows_ready = sem("f_rows")
        sent = sem("f_sent"); zeroed = sem("f_zeroed")
        h_filled = sem("f_h_filled"); h_act = sem("f_h_act"); h_ready = sem("f_h_ready")
        b2_added = sem("f_b2_added"); acc_free = sem("f_acc_free")
        y_done = sem("f_y"); act_past = sem("f_act_past"); sp_past = sem("f_sp_past")

        block = ctx.enter_context(nc.Block())
        pieces = [(w1_hi, w1_lo, "sh1T", c) for c in range(2)] + [(w2_hi, w2_lo, "sh2T", c) for c in range(2)]

        def piece(t, c):
            return t[:, :, :].rearrange("p a b -> p (a b)")[:, c * SH:(c + 1) * SH]

        def stage(n):
            at = n % 2 * SH
            return scratch[:, at:at + SH]


        @block.sync
        def _(sp):
            for name, dst in (("pw", pw_raw), ("pb_eb", pb_eb), ("experts", experts)):
                sp.dma_start(dst[:, :, :], dram[name]).then_inc(small_in, 16)
            for name, dst in (("tri", tri_f), ("token", token), ("sh1_b", b1)):
                sp.dma_start(dst[:, :], dram[name]).then_inc(small_in, 16)
            sp.dma_start(b2_row[:, :], dram["sh2_b"].partition_broadcast(P)).then_inc(small_in, 16)
            for n, (hi, lo, name, c) in enumerate(pieces):
                if n >= 2:
                    sp.wait_ge(w_done, n - 1)
                sp.dma_start(stage(n), dram[name][:, c * SH:(c + 1) * SH]).then_inc(w_staged[n % 2], 16)
            sp.wait_ge(const, 5)
            sp.dma_start(dram["slots"].rearrange("(p n) r -> p n r", p=P), zero_row[:, None, :].to_broadcast([P, E_N * CAP // P, ROW])).then_inc(zeroed, 16)
            ov = dram["out"].rearrange("b (c p) d -> p (b c) d", p=P)

            def write_out(s):
                sp.wait_ge(acc_free, s + 1)
                sp.sem_inc(sp_past, 1)
                sp.dma_start(ov[:, bass.ds(s * SUPER, SUPER), :], x_res[:, bass.ds(s * SUPER, SUPER), :]).then_inc(out_sem, 16)

            with sp.Fori(0, 5) as s:
                write_out(s)
            sp.wait_ge(slots_ready, 2)
            sp.dma_start(common["fc_raw"], dram["fcT"][0]).then_inc(common["fc_in"], 16)
            with sp.Fori(5, NS - 1) as s:
                write_out(s)
            sp.wait_ge(sent, 16 * 2 * NT)
            sp.dma_start(common["xe0"], dram["slots"][0:4 * P].rearrange("(t p) r -> p t r", p=P)).then_inc(common["xe0_in"], 16)
            write_out(NS - 1)

        @block.gpsimd
        def _(pool):
            pool.memset(eps_exp[:, 0], EPS)
            pool.memset(eps_exp[:, 1], -0.5).then_inc(const, 1)
            pool.memset(pw_hi[:, :, :].bitcast(F32), 0.0).then_inc(const, 1)
            pool.memset(pw_lo[:, :, :].bitcast(F32), 0.0).then_inc(const, 1)
            pool.memset(ones[:, :], 1.0).then_inc(const, 1)
            pool.memset(zero_row[:, :], 0.0).then_inc(const, 1)

            pool.wait_ge(const, 1)
            pool.wait_ge(pool_ln, 1)
            pool.tensor_tensor(var[:, :], var[:, :], eps_exp[:, 0], ALU.add).then_inc(pool_ln, 1)
            pool.wait_ge(pool_ln, 2)
            for at in (slice(0, 2 * SUPER), slice(2 * SUPER, NT)):
                pool.tensor_tensor(rstd[:, at], var[:, at], eps_exp[:, 1, at], ALU.pow).then_inc(rstd_ready, 1)

            def low_weights(pair):
                for n in (2 * pair, 2 * pair + 1):
                    hi, lo, name, c = pieces[n]
                    pool.wait_ge(w_high, n + 1)
                    pool.tensor_tensor(piece(lo, c), stage(n), piece(hi, c).bitcast(F32), ALU.subtract).then_inc(w_done, 1)

            def add_b2(start, end):
                with pool.Fori(start, end) as s:
                    pool.wait_ge(xs_ready, s + 1)
                    xb = x_res[:, bass.ds(s * SUPER, SUPER), :]
                    pool.tensor_tensor(xb, xb, b2_row[:, None, :].to_broadcast([P, SUPER, D]), ALU.add).then_inc(b2_added, 1)

            low_weights(0)
            add_b2(0, NS - 2)
            low_weights(1)
            add_b2(NS - 2, NS)
            with pool.Fori(0, SLOT_TURN // HB) as r:
                for b in range(HB):
                    pool.wait_ge(h_act, HB * r + b + 1)
                    pool.tensor_tensor(h_parts[:, b, 1], h_f[:, b % 2], h_parts[:, b, 0].bitcast(F32), ALU.subtract).then_inc(h_ready, 1)
            pool.wait_ge(rows_copied, NS)
            pool.wait_ge(rows_ready, 1)
            pool.wait_ge(slots_ready, 2)
            pool.wait_ge(zeroed, 16)
            for t in range(NT):
                for k in range(2):
                    pool.indirect_dma_start(out=dram["slots"], out_offset=bass.IndirectOffsetOnAxis(ap=slot[:, k, t:t + 1], axis=0),
                                            in_=rows[:, t, :], in_offset=None, bounds_check=E_N * CAP - 1, oob_is_err=False).then_inc(sent, 16)
            pool.wait_ge(sent, 16 * 2 * NT)

        @block.scalar
        def _(act):
            def iteration(s, n):
                if super_live(s):
                    for half in range(2):
                        act.wait_ge(t_filled, 2 * s + half + 1)
                        act.sem_inc(act_past, 1)
                        act.activation(xT_hi[:, :, bass.ds(s * SUPER * P + half * 2 * P, 2 * P)], bank_t[half][:, :, :], ACT.Identity).then_inc(xT_hi_ready, 1)
                if super_live(s - 1):
                    act.wait_ge(z_filled, s)
                    if super_live(s - 2):
                        act.wait_ge(zr_filled, s - 1)
                    act.activation(z_turn[:, :], bank_z[:, :], ACT.Identity).then_inc(z_copied, 1)
                if super_live(s):
                    act.wait_ge(xs_ready, s + 1)
                    act.sem_inc(act_past, 1)
                    act.activation(rows[:, bass.ds(s * SUPER, SUPER), 0:D], xs[n][:, :, :], ACT.Identity).then_inc(rows_copied, 1)
                if isinstance(s, int) and s in (0, NS - 2):
                    for m in ((0, 1) if s == 0 else (2, 3)):
                        hi, lo, name, c = pieces[m]
                        act.wait_ge(w_staged[m % 2], 16 * (m // 2 + 1))
                        act.activation(piece(hi, c), stage(m), ACT.Identity).then_inc(w_high, 1)

            super_tiles(act, iteration)
            act.wait_ge(sig_in, 1)
            act.activation(z[:, :, :], z[:, :, :], ACT.Sigmoid).then_inc(sig_done, 1)

            def hidden(s):
                for j in range(JC):
                    g = s * JC + j
                    act.wait_ge(h_filled, g + 1)
                    if not (isinstance(s, int) and g < 2):
                        act.wait_ge(h_ready, g - 1)
                    if not (isinstance(s, int) and g < HB):
                        act.wait_ge(y_done, g - HB + 1)
                    bank = bank_h[j % 2][:, :, :].rearrange("p a b -> p (a b)")
                    act.activation(h_parts[:, j % HB, 0], bank, ACT.Gelu, bias=b1[:, j:j + 1])
                    act.activation(h_f[:, j % 2], bank, ACT.Gelu, bias=b1[:, j:j + 1]).then_inc(h_act, 1)

            hidden(0)
            with act.Fori(1, NS) as s:
                hidden(s)

        @block.vector
        def _(dve):
            links = [0]

            def link(ins):
                links[0] += 1
                ins.then_inc(chain, 1)
                dve.wait_ge(chain, links[0])

            even, odd = stats[:, :, 1], stats[:, :, 4]
            dve.tensor_tensor(mu[:, :], even, odd, ALU.add)
            link(dve.tensor_tensor(dif[:, :], even, odd, ALU.subtract))
            dve.tensor_tensor(var[:, :], stats[:, :, 2], stats[:, :, 5], ALU.add)
            dve.tensor_scalar(mu[:, :], mu[:, :], 0.5, None, ALU.mult)
            link(dve.scalar_tensor_tensor(out=dif[:, :], in0=dif[:, :], scalar=0.25, in1=dif[:, :], op0=ALU.mult, op1=ALU.mult))
            dve.scalar_tensor_tensor(out=var[:, :], in0=var[:, :], scalar=1.0 / D, in1=dif[:, :], op0=ALU.mult, op1=ALU.add).then_inc(pool_ln, 1)
            dve.wait_ge(small_in, 7 * 16)
            dve.wait_ge(const, 5)
            dve.tensor_copy(tri[:, :], tri_f[:, :])
            link(dve.tensor_copy(pw_hi[:, :, 0:E_N], pw_raw[:, :, :]))
            dve.tensor_tensor(pw_lo[:, :, 0:E_N], pw_raw[:, :, :], pw_hi[:, :, 0:E_N].bitcast(F32), ALU.subtract).then_inc(pw_split, 1)
            dve.wait_ge(rstd_ready, 1)

            def layernorm(s, n):
                if super_live(s - 2):
                    dve.wait_ge(t_filled, 2 * (s - 1))
                    dve.wait_ge(rows_copied, s - 1)
                for j in range(SUPER):
                    t = s * SUPER + j
                    ins = dve.tensor_scalar(xs[n][:, j], x_res[:, bass.ds(t, 1), :].rearrange("p o d -> p (o d)"),
                                            mu[:, bass.ds(t, 1)], rstd[:, bass.ds(t, 1)], ALU.subtract, ALU.mult)
                ins.then_inc(xs_ready, 1)

            def router_iteration(s, n):
                if isinstance(s, int) and s == 1:
                    dve.wait_ge(rstd_ready, 2)
                if super_live(s + 1):
                    layernorm(s + 1, 1 - n)
                if super_live(s):
                    for half in range(2):
                        dve.wait_ge(xT_hi_ready, 2 * s + half + 1)
                        at = bass.ds(s * SUPER * P + half * 2 * P, 2 * P)
                        dve.tensor_tensor(xT_lo[:, :, at], bank_t[half][:, :, :], xT_hi[:, :, at].bitcast(F32), ALU.subtract).then_inc(xT_ready, 1)
                if super_live(s - 2):
                    dve.wait_ge(zr_filled, s - 1)
                    dve.tensor_tensor(z[:, :, bass.ds((s - 2) * SUPER, SUPER)], bank_r[:, :, 0:E_N].rearrange("p t e -> p e t"),
                                      pb_eb[:, 0, :, None].to_broadcast([P, E_N, SUPER]), ALU.add).then_inc(z_ready, 1)

            layernorm(0, 0)
            super_tiles(dve, router_iteration)

            dve.wait_ge(w_done, len(pieces))
            dve.wait_ge(z_ready, NS)
            dve.tensor_copy(g0[:, :, 0:1], z[:, :, 0:1]).then_inc(sig_in, 1)
            dve.wait_ge(sig_done, 1)

            def drain(s):
                dve.wait_ge(y_done, (s + 1) * JC)
                for m in range(SUPER // 2):
                    t = s * SUPER + 2 * m
                    ins = dve.tensor_tensor(x_res[:, t:t + 2], acc[s % 2][m][:, :, :], x_res[:, t:t + 2], ALU.add)
                ins.then_inc(acc_free, 1)

            def over_experts(t):
                return t[:, :, :].rearrange("p e t -> p t e")

            def each_token(t):
                return t[:, None, :].to_broadcast([P, E_N, NT])

            def each_expert(t):
                return t[:, :, None].to_broadcast([P, E_N, NT])

            best, norm, p0, p1, w0, w1 = (per_tok[:, n] for n in range(6))
            link(dve.tensor_tensor(z[:, :, :], z[:, :, :], each_expert(pb_eb[:, 1]), ALU.add))
            link(dve.tensor_scalar(z[:, :, :], z[:, :, :], 1e-12, None, ALU.max))
            link(dve.tensor_reduce(best, over_experts(z), AX_X, ALU.max))
            link(dve.reciprocal(norm, best))
            link(dve.tensor_tensor(z[:, :, :], z[:, :, :], each_token(norm), ALU.mult))
            link(dve.tensor_reduce(best, over_experts(z), AX_X, ALU.add))
            link(dve.reciprocal(norm, best))
            link(dve.tensor_tensor(prob[:, :, :], z[:, :, :], each_token(norm), ALU.mult))
            for n, (pick, p) in enumerate(((first, p0), (second, p1))):
                link(dve.tensor_reduce(p, over_experts(prob), AX_X, ALU.max))
                link(dve.tensor_tensor(g0[:, :, :], prob[:, :, :], each_token(p), ALU.is_equal))
                link(dve.tensor_tensor(g0[:, :, :], g0[:, :, :], each_expert(experts[:, 1]), ALU.mult))
                link(dve.tensor_reduce(best, over_experts(g0), AX_X, ALU.max))
                link(dve.tensor_tensor(pick[:, :, :], each_token(best), each_expert(experts[:, 1]), ALU.is_equal))
                if n == 0:
                    link(dve.scalar_tensor_tensor(out=prob[:, :, :], in0=first[:, :, :], scalar=-2.0, in1=prob[:, :, :], op0=ALU.mult, op1=ALU.add))
            link(dve.tensor_tensor(norm, p0, p1, ALU.add))
            link(dve.tensor_scalar(norm, norm, 1e-12, None, ALU.max))
            link(dve.reciprocal(norm, norm))
            dve.tensor_tensor(w0, p0, norm, ALU.mult)
            link(dve.tensor_tensor(w1, p1, norm, ALU.mult))
            dve.tensor_tensor(g0[:, :, :], first[:, :, :], each_token(w0), ALU.mult)
            link(dve.tensor_tensor(g1[:, :, :], second[:, :, :], each_token(w1), ALU.mult))
            dve.tensor_tensor(w_mask[:, :, :], first[:, :, :], second[:, :, :], ALU.add)
            link(dve.tensor_tensor(g0[:, :, :], g0[:, :, :], g1[:, :, :], ALU.add))
            link(dve.tensor_scalar(w_mask[:, :, :], w_mask[:, :, :], -1.0, None, ALU.add))
            link(dve.tensor_tensor(w_mask[:, :, :], w_mask[:, :, :], g0[:, :, :], ALU.add))
            dve.tensor_copy(rows[:, :, COL_W0], w0)
            dve.tensor_copy(rows[:, :, COL_W1], w1)
            dve.tensor_copy(rows[:, :, COL_TOK], token[:, :])
            dve.tensor_tensor(g0[:, :, :], first[:, :, :], each_expert(experts[:, 0]), ALU.mult)
            dve.memset(bound[:, :], 0).then_inc(search, 1)
            for n in range(CANDS):
                ins = dve.memset(step[:, n], (n + 1) << (BITS - BITS_STEP))
            link(ins)
            dve.tensor_reduce(rows[:, :, COL_E0], over_experts(g0), AX_X, ALU.add).then_inc(rows_ready, 1)

            dve.wait_ge(b2_added, NS)

            def search_steps(start, end):
                with dve.Fori(start, end) as r:
                    dve.wait_ge(search, STEP_INCS * r + 1)
                    dve.tensor_tensor(cand[:, :, :], bound[:, None, :].to_broadcast([P, CANDS, E_N]), step[:, :, :], ALU.bitwise_or).then_inc(search, 1)
                    dve.wait_ge(search, STEP_INCS * r + 2)
                    dve.tensor_tensor(reached[:, :, :, :], w_mask[:, None, :, :].to_broadcast([P, CANDS, E_N, NT]),
                                      cand[:, :, :, None].bitcast(F32).to_broadcast([P, CANDS, E_N, NT]), ALU.is_ge).then_inc(search, 1)
                    dve.wait_ge(search, STEP_INCS * r + 3)
                    with nc.allow_low_precision(reason="counts up to the 32 tiles are exact in bfloat16"):
                        dve.tensor_reduce(count[:, :].rearrange("p (c e) -> p c e", c=CANDS), reached[:, :, :, :], AX_X, ALU.add).then_inc(search, 1)
                    dve.wait_ge(counted, r + 1)
                    dve.tensor_scalar(over[:, :, :].rearrange("p c e -> p (c e)"), bank_z[:, 0:CANDS * E_N], float(CAP), None, ALU.is_ge).then_inc(search, 1)
                    for n in range(CANDS):
                        dve.wait_ge(search, STEP_INCS * r + 5 + n)
                        dve.tensor_scalar(step[:, n], step[:, n], BITS_STEP, None, ALU.logical_shift_right)
                        dve.copy_predicated(bound[:, :], over[:, n], cand[:, n]).then_inc(search, 1)

            search_steps(0, 6)
            drain(0)
            search_steps(6, 11)
            drain(1)
            search_steps(11, SEARCH_STEPS)
            drain(2)
            dve.wait_ge(search, STEP_INCS * SEARCH_STEPS + 1)
            limit = each_expert(bound[:, :].bitcast(F32))
            dve.tensor_tensor(kept[:, :, :], w_mask[:, :, :], limit, ALU.is_gt)
            link(dve.tensor_tensor(g1[:, :, :], w_mask[:, :, :], limit, ALU.is_equal))

            def before(mark, n):
                dve.tensor_copy(marks[:, :, :], mark[:, :, :]).then_inc(marked, 1)
                dve.wait_ge(summed, n + 1)
                for e in range(E_N):
                    ins = dve.tensor_tensor_scan(prob[:, e], ones[:, 0:NT], bank_z[:, e * NT:(e + 1) * NT], 0.0, ALU.mult, ALU.add)
                link(ins)
                totals = bank_z[:, 0:E_N * NT].rearrange("p (e t) -> p e t", e=E_N)
                inner = bank_r[:, :, :].rearrange("p a b -> p (a b)")[:, 0:E_N * NT].rearrange("p (e t) -> p e t", e=E_N)
                link(dve.tensor_tensor(g0[:, :, :], prob[:, :, :], totals, ALU.subtract))
                link(dve.tensor_tensor(g0[:, :, :], g0[:, :, :], inner, ALU.add))

            before(kept, 0)
            link(dve.tensor_scalar(room[:, :], prob[:, :, NT - 1], -1.0, float(CAP), ALU.mult, ALU.add))
            before(g1, 1)
            link(dve.tensor_tensor(g0[:, :, :], g0[:, :, :], each_expert(room[:, :]), ALU.is_lt))
            link(dve.tensor_tensor(g1[:, :, :], g1[:, :, :], g0[:, :, :], ALU.mult))
            link(dve.tensor_tensor(kept[:, :, :], kept[:, :, :], g1[:, :, :], ALU.add))
            before(kept, 2)
            link(dve.tensor_tensor(g0[:, :, :], g0[:, :, :], each_expert(experts[:, 2]), ALU.add))
            link(dve.scalar_tensor_tensor(out=g0[:, :, :], in0=kept[:, :, :], scalar=-float(FAR), in1=g0[:, :, :], op0=ALU.mult, op1=ALU.add))
            link(dve.tensor_scalar(g0[:, :, :], g0[:, :, :], float(FAR), None, ALU.add))
            for k, pick in enumerate((first, second)):
                link(dve.tensor_tensor(g1[:, :, :], g0[:, :, :], pick[:, :, :], ALU.mult))
                link(dve.tensor_reduce(slot_f[:, :], over_experts(g1), AX_X, ALU.add))
                dve.tensor_copy(slot[:, k], slot_f[:, :]).then_inc(slots_ready, 1)

            dve.wait_ge(h_ready, SLOT_TURN)
            drain(3)
            for g in range(SLOT_TURN, NS * JC):
                if g % JC == 3:
                    drain(g // JC - 1)
                dve.wait_ge(h_act, g + 1)
                dve.tensor_tensor(h_parts[:, g % HB, 1], h_f[:, g % 2], h_parts[:, g % HB, 0].bitcast(F32), ALU.subtract).then_inc(h_ready, 1)
            drain(NS - 1)

        @block.tensor
        def _(pe):
            def three(out, terms, start=True, stop=True):
                n, k = len(terms) * 3, 0
                for (lh, ll), (rh, rl) in terms:
                    for lhs, rhs in ((lh, rh), (lh, rl), (ll, rh)):
                        ins = pe.matmul(out, lhs, rhs, start=start and k == 0, stop=stop and k == n - 1)
                        k += 1
                return ins

            pe.wait_ge(small_in, 7 * 16)
            pe.wait_ge(const, 5)

            def router_iteration(s, n):
                if super_live(s):
                    pe.wait_ge(xs_ready, s + 1)
                    for half in range(2):
                        if super_live(s - 1):
                            pe.wait_ge(xT_ready, 2 * s + half - 1)
                        for c in range(DCH):
                            for j in range(2):
                                ins = pe.transpose(bank_t[half][:, c, j * P:(j + 1) * P], xs[n][:, 2 * half + j, c * P:(c + 1) * P], ident[:, :])
                        ins.then_inc(t_filled, 1)
                if super_live(s - 2):
                    pe.wait_ge(z_copied, s - 1)
                    if super_live(s - 3):
                        pe.wait_ge(z_ready, s - 2)
                    for j in range(SUPER):
                        ins = pe.transpose(bank_r[:, j, :], z_turn[:, j * P:(j + 1) * P], ident[:, :])
                    ins.then_inc(zr_filled, 1)
                if super_live(s - 1):
                    pe.wait_ge(xT_ready, 2 * s)
                    at = bass.ds((s - 1) * SUPER * P, SUPER * P)
                    three(bank_z[:, :], [((pw_hi[:, c], pw_lo[:, c]), (xT_hi[:, c, at], xT_lo[:, c, at])) for c in range(DCH)]).then_inc(z_filled, 1)

            pe.wait_ge(pw_split, 1)
            super_tiles(pe, router_iteration)
            pe.wait_ge(w_done, len(pieces))

            def up(g):
                s, j = g // JC, g % JC
                if g >= 2:
                    pe.wait_ge(h_act, g - 1)
                at = slice(s * SUPER * P, (s + 1) * SUPER * P)
                three(bank_h[j % 2][:, :, :].rearrange("p a b -> p (a b)"),
                      [((w1_hi[:, c, j * P:(j + 1) * P], w1_lo[:, c, j * P:(j + 1) * P]), (xT_hi[:, c, at], xT_lo[:, c, at])) for c in range(DCH)]).then_inc(h_filled, 1)

            def down(g):
                s, j = g // JC, g % JC
                pe.wait_ge(h_ready, g + 1)
                if j == 0 and s >= 2:
                    pe.wait_ge(acc_free, s - 1)
                for tt in range(SUPER):
                    cols = slice(tt * P, (tt + 1) * P)
                    for q, (part, w2) in enumerate(((0, w2_hi), (0, w2_lo), (1, w2_hi))):
                        ins = pe.matmul(acc[s % 2][tt // 2][:, tt % 2], h_parts[:, g % HB, part, cols], w2[:, j], start=(j == 0 and q == 0 and tt % 2 == 0),
                                        stop=(j == JC - 1 and q == 2), skip_group_check=True)
                ins.then_inc(y_done, 1)

            for half in range(2 * NS * JC):
                g = half // 2
                if half % 2 == 0:
                    up(g)
                elif g >= 2:
                    down(g - 2)
                if half in HALF_SEARCH:
                    r = HALF_SEARCH.index(half)
                    if r == 0:
                        pe.wait_ge(rows_ready, 1)
                    pe.wait_ge(search, STEP_INCS * r + 4)
                    pe.matmul(bank_z[:, 0:CANDS * E_N], ones[:, :], count[:, :], start=True, stop=True).then_inc(counted, 1)
                if half in HALF_SUMS:
                    pe.wait_ge(marked, HALF_SUMS.index(half) + 1)
                    flat = marks[:, :, :].rearrange("p e t -> p (e t)")
                    pe.matmul(bank_z[:, 0:E_N * NT], ones[:, :], flat, start=True, stop=True)
                    pe.matmul(bank_r[:, :, :].rearrange("p a b -> p (a b)")[:, 0:E_N * NT], tri[:, :], flat, start=True, stop=True).then_inc(summed, 1)
            down(NS * JC - 2)
            down(NS * JC - 1)


def run_experts(nc, ctx0, dram, common):
    JC = EH // P
    BATCHES = [(0, 4), (4, 4), (8, 2)]
    CH = len(BATCHES)
    BODY = 2 * CH
    BODIES = E_N // 2
    with ExitStack() as ctx:
        def sb(name, shape, dt=F32):
            return ctx.enter_context(nc.sbuf_tensor(name, shape, dt))

        def psum(name, shape):
            return ctx.enter_context(nc.psum_tensor(name, shape, F32))

        def sem(name):
            return ctx0.enter_context(nc.semaphore(name))

        ident, experts = common["ident"], common["experts"]
        b1 = [sb(f"fc1_b{n}", [P, JC]) for n in range(2)]
        w_raw = common["fc_raw"]
        w_hi = [sb(f"fc_hi{n}", [P, 2, DCH * EH], F32R) for n in range(2)]
        w_lo = [sb(f"fc_lo{n}", [P, 2, DCH * EH], F32R) for n in range(2)]
        b2_row = [sb(f"fc2_b{n}", [P, D]) for n in range(2)]
        xe = [common["xe0"], sb("xe1", [P, 4, ROW])]
        xeT_hi = [sb(f"xeT_hi{n}", [P, DCH, 4 * P], F32R) for n in range(2)]
        xeT_lo = [sb(f"xeT_lo{n}", [P, DCH, 4 * P], F32R) for n in range(2)]
        mine = sb("mine", [P, 4]); other = sb("other", [P, 4]); part0 = sb("part0", [P, 4]); part1 = sb("part1", [P, 4])
        weight = [sb(f"weight{n}", [P, 4]) for n in range(3)]
        away = sb("away", [P, 4]); tok_f = sb("tok_f", [P, 4])
        tok = [sb(f"tok{n}", [P, 4], U32) for n in range(3)]
        h_f = [sb(f"e_h_f{n}", [P, 4 * P]) for n in range(2)]
        h_hi = [sb(f"e_h_hi{n}", [P, 4 * P], F32R) for n in range(3)]
        h_lo = [sb(f"e_h_lo{n}", [P, 4 * P], F32R) for n in range(3)]
        y = [sb(f"y{n}", [P, 4, D]) for n in range(2)]
        y_w = [sb(f"y_w{n}", [P, 4, D]) for n in range(2)]

        bank_t = [psum(f"e_bank_t{n}", [P, DCH, 2 * P]) for n in range(2)]
        bank_h = [psum(f"e_bank_h{n}", [P, 4 * P]) for n in range(2)]
        acc = [[psum(f"e_acc{n}{i}", [P, 2, D]) for i in range(2)] for n in range(2)]

        w_in = common["fc_in"]; b2_in = [sem("e_b2_0"), sem("e_b2_1")]
        b1_in = [sem("e_b1_0"), sem("e_b1_1")]
        sp_past = sem("e_sp_past"); pool_past = sem("e_pool_past")
        w_high = sem("e_w_high"); w_ready = sem("e_w_ready"); w1_first = sem("e_w1_first")
        xe_in = [common["xe0_in"], sem("e_xe1")]
        t_filled = sem("e_t_filled"); t_high = sem("e_t_high"); t_ready = sem("e_t_ready")
        picked = sem("e_picked"); slot_info = sem("e_slot_info")
        h_filled = sem("e_h_filled"); h_act = sem("e_h_act"); h_high = sem("e_h_high"); h_ready = sem("e_h_ready")
        y_done = sem("e_y_done"); y_sum = sem("e_y_sum"); y_ready = sem("e_y_ready")
        added = [sem("e_added0"), sem("e_added1")]

        def chunks_before(k, m, p):
            return CH * k + sum(1 for q in range(m) if q % 2 == p)

        def tiles_through(k, m):
            if m < 0:
                k, m = k - 1, m + BODY
            per_body = sum(BATCHES[q % CH][1] for q in range(m % 2, BODY, 2))
            return per_body * k + sum(BATCHES[q % CH][1] for q in range(m % 2, m + 1, 2))

        def bodies(eng, body):
            body(0)
            with eng.Fori(1, BODIES - 1) as k:
                body(k)
            body(BODIES - 1)

        def ring(m, j):
            return (JC * m + j) % 3

        def precedes(k, m):
            if m:
                return k, m - 1
            return None if isinstance(k, int) and k == 0 else (k - 1, BODY - 1)

        def follows(k, m, ahead):
            if m + ahead < BODY:
                return k, m + ahead
            if isinstance(k, int) and k == BODIES - 1:
                return None
            return k + 1, m + ahead - BODY

        block = ctx.enter_context(nc.Block())

        @block.sync
        def _(sp):
            def load_weights(e, n):
                if not (isinstance(e, int) and e == 0):
                    sp.dma_start(w_raw[:, :, :], dram["fcT"][bass.ds(e, 1)].rearrange("o p a b -> p (o a) b")).then_inc(w_in, 16)
                sp.dma_start(b2_row[n][:, :], dram["fc2_b"][bass.ds(e, 1)].rearrange("o d -> (o d)").partition_broadcast(P)).then_inc(b2_in[n], 16)
                sp.dma_start(b1[n][:, :], dram["fc1_b"][bass.ds(e, 1)].rearrange("o p j -> p (o j)")).then_inc(b1_in[n], 16)

            def load_chunk(k, m):
                e = 2 * k + m // CH
                first, tiles = BATCHES[m % CH]
                src = dram["slots"].rearrange("(e t p) r -> p (e t) r", e=E_N, p=P)[:, bass.ds(e * (CAP // P) + first, tiles)]
                sp.dma_start(xe[m % 2][:, 0:tiles], src).then_inc(xe_in[m % 2], 16)

            load_weights(0, 0)
            load_chunk(0, 1)

            def body(k):
                for m in range(BODY):
                    n = BODY * k + m
                    if m % CH == 0:
                        e = 2 * k + m // CH
                        if follows(k, m, CH):
                            if isinstance(n, int) and n == 0:
                                sp.wait_ge(w_ready, 1)
                                sp.wait_ge(w1_first, 2)
                            else:
                                sp.wait_ge(y_sum, n)
                            sp.sem_inc(sp_past, 1)
                            load_weights(e + 1, (m // CH + 1) % 2)
                    nxt = follows(k, m, 2)
                    if nxt:
                        sp.wait_ge(t_filled, n + 1)
                        sp.wait_ge(slot_info, n + 1)
                        sp.sem_inc(sp_past, 1)
                        load_chunk(*nxt)

            bodies(sp, body)

        @block.gpsimd
        def _(pool):
            def low_weights(e, n):
                pool.wait_ge(w_high, e + 1)
                pool.tensor_tensor(w_lo[n][:, :, :], w_raw[:, :, :], w_hi[n][:, :, :].bitcast(F32), ALU.subtract).then_inc(w_ready, 1)

            pool.wait_ge(w_high, 1)
            pool.tensor_tensor(w_lo[0][:, 1], w_raw[:, 1], w_hi[0][:, 1].bitcast(F32), ALU.subtract).then_inc(w_ready, 1)
            pool.wait_ge(common["x_out"], 16 * NS)

            def body(k):
                for m in range(BODY):
                    n = BODY * k + m
                    if m % CH == 1 and follows(k, m, CH):
                        low_weights(2 * k + m // CH + 1, (m // CH + 1) % 2)
                    pool.wait_ge(y_ready, n + 1)
                    pool.sem_inc(pool_past, 1)
                    for j in range(BATCHES[m % CH][1]):
                        pool.indirect_dma_start(out=dram["out"].rearrange("b s d -> (b s) d"), out_offset=bass.IndirectOffsetOnAxis(ap=tok[m % 3][:, j:j + 1], axis=0),
                                                in_=y_w[m % 2][:, j, :], in_offset=None, bounds_check=N_TOK - 1, oob_is_err=False,
                                                compute_op=ALU.add).then_inc(added[m % 2], 16)
                    if m % CH == CH - 1:
                        pool.wait_ge(added[m % 2], 16 * tiles_through(k, m))
                        pool.wait_ge(added[1 - m % 2], 16 * tiles_through(k, m - 1))

            bodies(pool, body)

        @block.scalar
        def _(act):
            def high(k, m):
                n = BODY * k + m
                tiles = BATCHES[m % CH][1]
                act.wait_ge(t_filled, n + 1)
                if not (isinstance(n, int) and n < 2):
                    act.wait_ge(h_filled, JC * (n - 1))
                for half in range(tiles // 2):
                    ins = act.activation(xeT_hi[m % 2][:, :, half * 2 * P:(half + 1) * 2 * P], bank_t[half][:, :, :], ACT.Identity)
                ins.then_inc(t_high, 1)

            high(0, 0)

            def body(k):
                for m in range(BODY):
                    n = BODY * k + m
                    cols = BATCHES[m % CH][1] * P
                    act.wait_ge(b1_in[m // CH], 16 * (k + 1))
                    for j in range(JC):
                        act.wait_ge(h_filled, JC * n + j + 1)
                        if j >= 2 or precedes(k, m):
                            act.wait_ge(h_ready, JC * n + j - 1)
                        act.activation(h_f[j % 2][:, 0:cols], bank_h[j % 2][:, 0:cols], ACT.Gelu,
                                       bias=b1[m // CH][:, j:j + 1]).then_inc(h_act, 1)
                        if j == 1 and follows(k, m, 1):
                            high(*follows(k, m, 1))

            bodies(act, body)

        @block.vector
        def _(dve):
            def high_weights(e, n):
                dve.wait_ge(w_in, 16 * (e + 1))
                dve.tensor_copy(w_hi[n][:, :, :], w_raw[:, :, :]).then_inc(w_high, 1)

            def low(k, m):
                n = BODY * k + m
                tiles = BATCHES[m % CH][1]
                dve.wait_ge(t_high, n + 1)
                for half in range(tiles // 2):
                    at = slice(half * 2 * P, (half + 1) * 2 * P)
                    ins = dve.tensor_tensor(xeT_lo[m % 2][:, :, at], bank_t[half][:, :, :], xeT_hi[m % 2][:, :, at].bitcast(F32), ALU.subtract)
                ins.then_inc(t_ready, 1)

            def slot_values(k, m):
                n = BODY * k + m
                e = 2 * k + m // CH
                t = BATCHES[m % CH][1]
                src = xe[m % 2]
                PICKS = 4
                dve.wait_ge(xe_in[m % 2], 16 * (chunks_before(k, m, m % 2) + 1))
                dve.tensor_scalar(mine[:, 0:t], src[:, 0:t, COL_E0], experts[:, 0, bass.ds(e, 1)], None, ALU.is_equal)
                dve.tensor_scalar(away[:, 0:t], src[:, 0:t, COL_TOK], 0.0, float(FAR), ALU.is_equal, ALU.mult).then_inc(picked, 1)
                dve.wait_ge(picked, PICKS * n + 1)
                dve.tensor_scalar(other[:, 0:t], mine[:, 0:t], -1.0, 1.0, ALU.mult, ALU.add)
                dve.tensor_tensor(part0[:, 0:t], src[:, 0:t, COL_W0], mine[:, 0:t], ALU.mult)
                dve.scalar_tensor_tensor(out=tok_f[:, 0:t], in0=src[:, 0:t, COL_TOK], scalar=-1.0, in1=away[:, 0:t], op0=ALU.add, op1=ALU.add).then_inc(picked, 1)
                dve.wait_ge(picked, PICKS * n + 2)
                dve.tensor_tensor(part1[:, 0:t], src[:, 0:t, COL_W1], other[:, 0:t], ALU.mult).then_inc(picked, 1)
                if not (isinstance(n, int) and n < 3):
                    dve.wait_ge(added[(m - 3) % 2], 16 * tiles_through(k, m - 3))
                dve.tensor_copy(tok[m % 3][:, 0:t], tok_f[:, 0:t]).then_inc(picked, 1)
                dve.wait_ge(picked, PICKS * n + 4)
                dve.tensor_tensor(weight[m % 3][:, 0:t], part0[:, 0:t], part1[:, 0:t], ALU.add).then_inc(slot_info, 1)

            dve.wait_ge(w_in, 16)
            dve.tensor_copy(w_hi[0][:, 0], w_raw[:, 0]).then_inc(w1_first, 1)
            dve.tensor_copy(w_hi[0][:, 1], w_raw[:, 1]).then_inc(w_high, 1)
            dve.wait_ge(w1_first, 1)
            dve.tensor_tensor(w_lo[0][:, 0], w_raw[:, 0], w_hi[0][:, 0].bitcast(F32), ALU.subtract).then_inc(w1_first, 1)
            low(0, 0)
            slot_values(0, 0)

            def send(k, m):
                n = BODY * k + m
                tiles = BATCHES[m % CH][1]
                dve.wait_ge(b2_in[m // CH], 16 * (k + 1))
                dve.wait_ge(y_done, JC * (n + 1))
                for i in range(tiles // 2):
                    ins = dve.tensor_tensor(y[m % 2][:, 2 * i:2 * i + 2], acc[m % 2][i][:, :, :], b2_row[m // CH][:, None, :].to_broadcast([P, 2, D]), ALU.add)
                ins.then_inc(y_sum, 1)
                dve.wait_ge(y_sum, n + 1)
                dve.wait_ge(slot_info, n + 1)
                if not (isinstance(n, int) and n < 2):
                    dve.wait_ge(added[m % 2], 16 * tiles_through(k, m - 2))
                for j in range(tiles):
                    ins = dve.tensor_scalar(y_w[m % 2][:, j], y[m % 2][:, j], weight[m % 3][:, j:j + 1], None, ALU.mult)
                ins.then_inc(y_ready, 1)

            def body(k):
                for m in range(BODY):
                    n = BODY * k + m
                    cols = BATCHES[m % CH][1] * P
                    for j in range(JC):
                        b = ring(m, j)
                        dve.wait_ge(h_act, JC * n + j + 1)
                        if j == 3 or precedes(k, m):
                            dve.wait_ge(y_done, JC * n + j - 2)
                        dve.tensor_copy(h_hi[b][:, 0:cols], h_f[j % 2][:, 0:cols]).then_inc(h_high, 1)
                        dve.wait_ge(h_high, JC * n + j + 1)
                        dve.tensor_tensor(h_lo[b][:, 0:cols], h_f[j % 2][:, 0:cols], h_hi[b][:, 0:cols].bitcast(F32), ALU.subtract).then_inc(h_ready, 1)
                        if j == 1:
                            if follows(k, m, 1):
                                low(*follows(k, m, 1))
                            if precedes(k, m):
                                send(*precedes(k, m))
                            if follows(k, m, 1):
                                slot_values(*follows(k, m, 1))
                        if j == 2 and m % CH == 1 and follows(k, m, CH):
                            high_weights(2 * k + m // CH + 1, (m // CH + 1) % 2)

            bodies(dve, body)
            send(BODIES - 1, BODY - 1)

        @block.tensor
        def _(pe):
            def three(out, terms, start=True, stop=True):
                n, k = len(terms) * 3, 0
                for (lh, ll), (rh, rl) in terms:
                    for lhs, rhs in ((lh, rh), (lh, rl), (ll, rh)):
                        ins = pe.matmul(out, lhs, rhs, start=start and k == 0, stop=stop and k == n - 1)
                        k += 1
                return ins

            def turn(k, m):
                tiles = BATCHES[m % CH][1]
                pe.wait_ge(xe_in[m % 2], 16 * (chunks_before(k, m, m % 2) + 1))
                for half in range(tiles // 2):
                    for c in range(DCH):
                        for j in range(2):
                            ins = pe.transpose(bank_t[half][:, c, j * P:(j + 1) * P], xe[m % 2][:, 2 * half + j, c * P:(c + 1) * P], ident[:, :])
                ins.then_inc(t_filled, 1)

            turn(0, 0)

            def up(k, m, j):
                n = BODY * k + m
                f, cols = m // CH, BATCHES[m % CH][1] * P
                if j == 0:
                    pe.wait_ge(t_ready, n + 1)
                    if isinstance(n, int) and n == 0:
                        pe.wait_ge(w1_first, 2)
                    else:
                        pe.wait_ge(w_ready, 2 * k + f + 1)
                if j >= 2 or precedes(k, m):
                    pe.wait_ge(h_act, JC * n + j - 1)
                w = [slice(c * EH + j * P, c * EH + (j + 1) * P) for c in range(DCH)]
                three(bank_h[j % 2][:, 0:cols], [((w_hi[f][:, 0, w[c]], w_lo[f][:, 0, w[c]]), (xeT_hi[m % 2][:, c, 0:cols], xeT_lo[m % 2][:, c, 0:cols])) for c in range(DCH)]).then_inc(h_filled, 1)

            def down(k, m, j):
                n = BODY * k + m
                f, tiles = m // CH, BATCHES[m % CH][1]
                pe.wait_ge(h_ready, JC * n + j + 1)
                if j == 0 and isinstance(n, int) and n == 0:
                    pe.wait_ge(w_ready, 1)
                if j == 0 and not (isinstance(n, int) and n < 2):
                    pe.wait_ge(y_sum, n - 1)
                b = ring(m, j)
                wd = slice(j * D, (j + 1) * D)
                for tt in range(tiles):
                    at = slice(tt * P, (tt + 1) * P)
                    for q, (lhs, rhs) in enumerate(((h_hi, w_hi), (h_hi, w_lo), (h_lo, w_hi))):
                        ins = pe.matmul(acc[m % 2][tt // 2][:, tt % 2], lhs[b][:, at], rhs[f][:, 1, wd], start=(j == 0 and q == 0 and tt % 2 == 0),
                                        stop=(j == JC - 1 and q == 2), skip_group_check=True)
                ins.then_inc(y_done, 1)

            def body(k):
                for m in range(BODY):
                    for j in range(JC):
                        up(k, m, j)
                        if j == 1 and follows(k, m, 1):
                            turn(*follows(k, m, 1))
                        if j >= 2:
                            down(k, m, j - 2)
                        elif precedes(k, m):
                            down(*precedes(k, m), JC + j - 2)

            bodies(pe, body)
            down(BODIES - 1, BODY - 1, JC - 2)
            down(BODIES - 1, BODY - 1, JC - 1)


def moe_block(nc, dram):
    with ExitStack() as ctx:
        def sb(name, shape, dt=F32):
            return ctx.enter_context(nc.sbuf_tensor(name, shape, dt))

        x_res = sb("x_res", [P, NT, D])
        res_stats = sb("res_stats", [P, NT, 6])
        fc_raw_size, xe_size = 2 * DCH * EH, 4 * ROW
        scratch = sb("scratch", [P, (8 + CANDS) * E_N * NT + SUPER * P])
        common = {
            "ident": sb("ident", [P, P]),
            "experts": sb("experts", [P, 3, E_N]),
            "scratch": scratch,
            "fc_raw": scratch[:, 0:fc_raw_size].rearrange("p (a b) -> p a b", a=2),
            "xe0": scratch[:, fc_raw_size:fc_raw_size + xe_size].rearrange("p (t r) -> p t r", t=4),
            "fc_in": ctx.enter_context(nc.semaphore("fc_in")),
            "xe0_in": ctx.enter_context(nc.semaphore("xe0_in")),
            "x_out": ctx.enter_context(nc.semaphore("x_out")),
        }
        attention(nc, ctx, dram, x_res, res_stats, common)
        route_and_shared(nc, ctx, dram, x_res, res_stats, common)
        run_experts(nc, ctx, dram, common)


def kernel(**inputs):
    import concourse.bacc as bacc
    from concourse.bass_utils import run_bass_kernel_spmd

    att = {k[len("L0_xcond_"):]: np.asarray(v) for k, v in inputs.items() if k.startswith("L0_xcond_")}
    ffn = {k[len("L0_ffn_"):]: np.asarray(v) for k, v in inputs.items() if k.startswith("L0_ffn_")}
    sel, one_rows, ident = consts()
    tri, experts, token = route_consts()

    def columns(w, chunks):
        return w.reshape(w.shape[0], chunks, P).transpose(2, 1, 0)

    fc1 = ffn["fc1_w"].reshape(E_N, EH, DCH, P).transpose(0, 3, 2, 1).reshape(E_N, P, DCH * EH)
    fc2 = ffn["fc2_w"].reshape(E_N, D, EH // P, P).transpose(0, 3, 2, 1).reshape(E_N, P, EH // P * D)
    arrays = {
        "x": inputs["x"],
        "ctxT": np.transpose(np.asarray(inputs["ctx_1024"]), (0, 2, 1)),
        "tau": inputs["condB_tau"],
        "delta": inputs["fside_BxS2_0"],
        "WqT": att["Wq"].T, "WkT": att["Wk"].T, "WvT": att["Wv"].T, "WoT": att["Wo"].T,
        "b_qk": np.stack([att["bq"], att["bk"]]).reshape(2, DCH, P).transpose(2, 0, 1),
        "bv": att["bv"], "bo": att["bo"],
        "sel": sel, "one_rows": one_rows, "ident": ident,
        "pw": columns(ffn["proj_w"], DCH),
        "pb_eb": np.broadcast_to(np.stack([ffn["proj_b"], ffn["expert_bias"]])[None], (P, 2, E_N)),
        "sh1T": columns(ffn["sh1_w"], DCH).reshape(P, DCH * SH),
        "sh1_b": ffn["sh1_b"].reshape(SH // P, P).T,
        "sh2T": columns(ffn["sh2_w"], SH // P).reshape(P, SH // P * D),
        "sh2_b": ffn["sh2_b"],
        "fcT": np.stack([fc1, fc2], axis=2),
        "fc1_b": ffn["fc1_b"].reshape(E_N, EH // P, P).transpose(0, 2, 1),
        "fc2_b": ffn["fc2_b"],
        "tri": tri, "experts": experts, "token": token,
    }
    nc = bacc.Bacc("TRN2", target_bir_lowering=False, num_devices=1)
    given, dram = {}, {}
    for name, a in arrays.items():
        a = np.ascontiguousarray(a)
        given[f"in_{name}_dram"] = a
        dram[name] = nc.dram_tensor(f"in_{name}_dram", a.shape, mybir.dt.from_np(a.dtype), kind="ExternalInput").ap()
    dram["delta_hl"] = nc.dram_tensor("delta_hl_dram", (B, 2, S), F32, kind="Internal").ap()
    dram["slots"] = nc.dram_tensor("slots_dram", (E_N * CAP, ROW), F32, kind="Internal").ap()
    dram["out"] = nc.dram_tensor("out_dram", (B, S, D), F32, kind="ExternalOutput").ap()
    moe_block(nc, dram)
    r = run_bass_kernel_spmd(nc, [given], core_ids=[0])
    return r.results[0]["out_dram"]
```
